# Optimizing a Trainium2 kernel written in Bass

```python
import numpy as np
import jax
import jax.numpy as jnp

def _softmax(x, axis=-1):
    return jax.nn.softmax(x, axis=axis)

def _gelu(x):
    return jax.nn.gelu(x, approximate=True)

def _silu(x):
    return jax.nn.silu(x)

def _sigmoid(x):
    return jax.nn.sigmoid(x)

def _layernorm(x, axis=-1, eps=1e-05):
    m = jnp.mean(x, axis=axis, keepdims=True)
    v = jnp.var(x, axis=axis, keepdims=True)
    return (x - m) / jnp.sqrt(v + eps)

def _scatter_add(tgt, idx, src, axis=0):
    return tgt.at[idx].add(src)

def _segment_sum(src, seg, n):
    return jax.ops.segment_sum(src, seg, n)
kernel_name = 'mk_hybrid_d1_jaxref_r8_8915b7'

def setup_inputs(seed: int=0):
    np.random.seed(seed)
    _w = jnp.asarray

    def _L0_attn_a_setup():
        import jax, jax.numpy as jnp
        import numpy as np
        B, S, D, H = (4, 256, 128, 16)
        key = jax.random.key(seed)
        k1, k2, k3 = jax.random.split(key, 3)
        x = jax.random.normal(k1, (B, S, D), dtype=jnp.float32)
        w1 = jax.random.normal(k2, (D, 3 * D), dtype=jnp.float32) * (1.0 / np.sqrt(D))
        b1 = jnp.zeros((3 * D,), dtype=jnp.float32)
        w2 = jax.random.normal(k3, (D, D), dtype=jnp.float32) * (1.0 / np.sqrt(D))
        b2 = jnp.zeros((D,), dtype=jnp.float32)
        return {'x': x, 'w1': w1, 'b1': b1, 'w2': w2, 'b2': b2}
    _L0_attn_a_in = _L0_attn_a_setup()

    def _L0_attn_b_setup():
        import jax, jax.numpy as jnp
        import numpy as np
        import math
        D_MODEL = 128
        NUM_HEADS = 16
        THETA = 10000.0

        def _rope(x, theta):
            n, d_k = (x.shape[-2], x.shape[-1])
            powers = jnp.arange(0, d_k, 2, dtype=jnp.float32) / d_k
            freqs = 1.0 / theta ** powers
            t = jnp.arange(n, dtype=jnp.float32)
            angles = jnp.outer(t, freqs)
            cos = jnp.cos(angles).astype(x.dtype)
            sin = jnp.sin(angles).astype(x.dtype)
            x_even = x[..., 0::2]
            x_odd = x[..., 1::2]
            rot_even = x_even * cos - x_odd * sin
            rot_odd = x_even * sin + x_odd * cos
            return jnp.stack([rot_even, rot_odd], axis=-1).reshape(x.shape)
        key = jax.random.key(seed)
        ks = jax.random.split(key, 5)
        B, N, D = (2, 256, D_MODEL)
        std = math.sqrt(2.0 / (D + D))
        x = jax.random.normal(ks[0], (B, N, D), dtype=jnp.float32)
        wq = jax.random.normal(ks[1], (D, D), dtype=jnp.float32) * std
        wk = jax.random.normal(ks[2], (D, D), dtype=jnp.float32) * std
        wv = jax.random.normal(ks[3], (D, D), dtype=jnp.float32) * std
        wo = jax.random.normal(ks[4], (D, D), dtype=jnp.float32) * std
        return {'x': x, 'wq': wq, 'wk': wk, 'wv': wv, 'wo': wo}
    _L0_attn_b_in = _L0_attn_b_setup()

    def _L0_ffn_setup():
        import jax, jax.numpy as jnp
        import numpy as np
        DIM = 128
        HIDDEN = 384
        SCALE = 1.0 / 127.0

        def _dequant(w_int, dtype):
            return w_int.astype(dtype) * jnp.asarray(SCALE, dtype)
        key = jax.random.key(seed)
        k_x, k_g, k_u, k_d = jax.random.split(key, 4)
        x = jax.random.normal(k_x, (4, 256, DIM), dtype=jnp.float32)
        w_gate = jax.random.randint(k_g, (HIDDEN, DIM), -127, 128, dtype=jnp.int32)
        w_up = jax.random.randint(k_u, (HIDDEN, DIM), -127, 128, dtype=jnp.int32)
        w_down = jax.random.randint(k_d, (DIM, HIDDEN), -127, 128, dtype=jnp.int32)
        return {'x': x, 'w_gate': w_gate, 'w_up': w_up, 'w_down': w_down}
    _L0_ffn_in = _L0_ffn_setup()
    _d = {'L0_attn_a_x': _L0_attn_a_in['x'], 'L0_attn_a_w1': _L0_attn_a_in['w1'], 'L0_attn_a_b1': _L0_attn_a_in['b1'], 'L0_attn_a_w2': _L0_attn_a_in['w2'], 'L0_attn_a_b2': _L0_attn_a_in['b2'], 'L0_attn_b_wq': _L0_attn_b_in['wq'], 'L0_attn_b_wk': _L0_attn_b_in['wk'], 'L0_attn_b_wv': _L0_attn_b_in['wv'], 'L0_attn_b_wo': _L0_attn_b_in['wo'], 'L0_ffn_w_gate': _L0_ffn_in['w_gate'], 'L0_ffn_w_up': _L0_ffn_in['w_up'], 'L0_ffn_w_down': _L0_ffn_in['w_down']}
    _x0 = _d['L0_attn_a_x']
    _d['L0_attn_a_x'] = jax.random.normal(jax.random.fold_in(jax.random.key(seed), 1), (8, 512, 128), dtype=_x0.dtype)
    del _x0
    return _d

def reference(L0_attn_a_x, L0_attn_a_w1, L0_attn_a_b1, L0_attn_a_w2, L0_attn_a_b2, L0_attn_b_wq, L0_attn_b_wk, L0_attn_b_wv, L0_attn_b_wo, L0_ffn_w_gate, L0_ffn_w_up, L0_ffn_w_down):

    def _L0_attn_a_ref(x, w1, b1, w2, b2):
        import jax, jax.numpy as jnp
        import numpy as np
        B, S, D, H = (4, 256, 128, 16)
        b, s, d = x.shape
        h = H
        dh = d // h
        qkv = jnp.einsum('bsd,de->bse', x, w1) + b1
        q, k, v = jnp.split(qkv, 3, axis=2)

        def sh(t):
            return t.reshape(b, s, h, dh).transpose(0, 2, 1, 3)
        q, k, v = (sh(q), sh(k), sh(v))
        w = jnp.einsum('bhqd,bhkd->bhqk', q, k)
        w = jax.nn.softmax(w, axis=-1)
        a = jnp.einsum('bhqk,bhkd->bhqd', w, v)
        a = a.transpose(0, 2, 1, 3).reshape(b, s, d)
        out = jnp.einsum('bsd,de->bse', a, w2) + b2
        return out

    def _L0_attn_b_ref(x, wq, wk, wv, wo):
        import jax, jax.numpy as jnp
        import numpy as np
        import math
        D_MODEL = 128
        NUM_HEADS = 16
        THETA = 10000.0

        def _rope(x, theta):
            n, d_k = (x.shape[-2], x.shape[-1])
            powers = jnp.arange(0, d_k, 2, dtype=jnp.float32) / d_k
            freqs = 1.0 / theta ** powers
            t = jnp.arange(n, dtype=jnp.float32)
            angles = jnp.outer(t, freqs)
            cos = jnp.cos(angles).astype(x.dtype)
            sin = jnp.sin(angles).astype(x.dtype)
            x_even = x[..., 0::2]
            x_odd = x[..., 1::2]
            rot_even = x_even * cos - x_odd * sin
            rot_odd = x_even * sin + x_odd * cos
            return jnp.stack([rot_even, rot_odd], axis=-1).reshape(x.shape)
        B, N, D = x.shape
        H = NUM_HEADS
        d_k = D // H

        def split_heads(t):
            return t.reshape(B, N, H, d_k).transpose(0, 2, 1, 3)
        Q = split_heads(x @ wq.T)
        K = split_heads(x @ wk.T)
        V = split_heads(x @ wv.T)
        Q = _rope(Q, THETA)
        K = _rope(K, THETA)
        scale = 1.0 / math.sqrt(d_k)
        scores = jnp.einsum('bhqd,bhkd->bhqk', Q, K) * scale
        causal_mask = jnp.triu(jnp.ones((N, N), dtype=bool), k=1)
        scores = jnp.where(causal_mask, -jnp.inf, scores)
        attn = jax.nn.softmax(scores, axis=-1)
        out = jnp.einsum('bhqk,bhkd->bhqd', attn, V)
        out = out.transpose(0, 2, 1, 3).reshape(B, N, D)
        return out @ wo.T

    def _L0_ffn_ref(x, w_gate, w_up, w_down):
        import jax, jax.numpy as jnp
        import numpy as np
        DIM = 128
        HIDDEN = 384
        SCALE = 1.0 / 127.0

        def _dequant(w_int, dtype):
            return w_int.astype(dtype) * jnp.asarray(SCALE, dtype)
        wg = _dequant(w_gate, x.dtype)
        wu = _dequant(w_up, x.dtype)
        wd = _dequant(w_down, x.dtype)
        gate = jnp.einsum('bsd,hd->bsh', x, wg)
        up = jnp.einsum('bsd,hd->bsh', x, wu)
        h = jax.nn.silu(gate) * up
        return jnp.einsum('bsh,dh->bsd', h, wd)
    x = L0_attn_a_x
    x = x + _L0_attn_a_ref(_layernorm(x, axis=-1), L0_attn_a_w1, L0_attn_a_b1, L0_attn_a_w2, L0_attn_a_b2)
    x = x + _L0_ffn_ref(_layernorm(x, axis=-1), L0_ffn_w_gate, L0_ffn_w_up, L0_ffn_w_down)
    x = x + _L0_attn_b_ref(_layernorm(x, axis=-1), L0_attn_b_wq, L0_attn_b_wk, L0_attn_b_wv, L0_attn_b_wo)
    x = x + _L0_ffn_ref(_layernorm(x, axis=-1), L0_ffn_w_gate, L0_ffn_w_up, L0_ffn_w_down)
    return x

_drawn_inputs = setup_inputs


def setup_inputs(seed=0):
    import zlib

    import numpy as np

    out = dict(_drawn_inputs(seed))
    spreads = {'L0_attn_a_b1': (0.0, 0.1), 'L0_attn_a_b2': (0.0, 0.1)}
    factors = {'L0_attn_b_wq': 8.0, 'L0_attn_b_wk': 8.0, 'L0_attn_b_wv': 8.0, 'L0_attn_b_wo': 8.0}
    for name, (base, spread) in spreads.items():
        noise = np.random.default_rng([zlib.crc32(name.encode()), seed]).standard_normal(out[name].shape)
        drawn = base * np.exp(spread * noise) if base else spread * noise
        out[name] = jnp.asarray(drawn.astype(out[name].dtype))
    for name, factor in factors.items():
        out[name] = (out[name] * factor).astype(out[name].dtype)
    return out
```

```python
from contextlib import ExitStack

import numpy as np
import concourse.bass as bass
from concourse import mybir

F32 = mybir.dt.float32
BF16 = mybir.dt.bfloat16
I32 = mybir.dt.int32
ACT = mybir.ActivationFunctionType
ALU = mybir.AluOpType
AX = mybir.AxisListType

NB, T, D, H = 8, 512, 128, 16
DH = D // H
HB = 3
TT = T // 128
G, J = 4, 4
QUADS = G * TT
EPS = 1e-5
PARTS = 3
HALF = DH // 2
PROD = 6 * DH
SH = 96
KROWS = SH + PARTS
BIG = -3.0e38
LA, LB = 0, 1
JOBS = 2 * NB
OROW = 32
SUMROW = DH

FRONT_A = {(0, 1): "norm_A", (1, 1): "qk_even_A", (2, 0): "qk_odd_A", (2, 1): "v_A"}
FRONT_B = {(3, 0): "norm_B", (4, 1): "qk_even_B", (5, 1): "qk_odd_B", (6, 0): "v_B"}
SHIFTS = {(1, 0): "shift0", (5, 0): "shift1", (9, 0): "shift2", (13, 0): "shift3"}
TAIL_IN_A = {(4, 0): "out_proj", (6, 1): "norm_mid", (7, 0): "gate0", (7, 1): "up0", (8, 0): "gate1",
             (8, 1): "up1", (9, 1): "gate2", (10, 0): "up2", (11, 0): "down"}
TAIL_IN_B = {(6, 1): "out_proj", (10, 0): "norm_mid", (10, 1): "gate0", (11, 0): "up0", (11, 1): "gate1",
             (12, 0): "up1", (12, 1): "gate2", (13, 1): "up2", (14, 1): "down"}
TAIL_ORDER = ["out_proj", "norm_mid", "gate0", "up0", "gate1", "up1", "gate2", "up2", "down"]


class Turn:

    def __init__(self, layer, t, t0):
        self.layer, self.t, self.t0 = layer, t, t0
        self.job, self.job0 = layer * NB + t, layer * NB + t0
        self.front_a = layer == LA and t0 + 2 < NB
        self.tail = self.job0 > 0
        self.front_b = 2 <= self.job0 < NB + 2
        self.b_a = t + 2
        self.b_b = self.job - 2
        prev = self.job - 1
        self.tail_layer = LA if self.job0 <= NB else LB
        self.tail_b = prev - self.tail_layer * NB
        steps = dict(SHIFTS)
        if self.job0 == JOBS - 1:
            del steps[(13, 0)]
        if self.front_a:
            steps.update(FRONT_A)
        if self.tail:
            steps.update(TAIL_IN_A if layer == LA else TAIL_IN_B)
        if self.front_b:
            steps.update(FRONT_B)
        self.steps = steps
        self.order = {name: i for i, (_, name) in enumerate(sorted(steps.items()))}

    def number(self, name):
        base = PROLOGUE_STEPS
        for job in range(self.job0):
            base += len(Turn(job // NB, job % NB, job % NB).order)
        return base + self.order[name] + len(self.order) * (self.t - self.t0)

    def group_after(self, g, ahead):
        if g + ahead < G:
            return self.layer, self.t, g + ahead
        if self.job0 == JOBS - 1:
            return None
        if self.layer == LA and self.t0 == NB - 1:
            return LB, 0, g + ahead - G
        return self.layer, self.t + 1, g + ahead - G


class LastTail:
    job, tail_layer, tail_b = JOBS, LB, NB - 1

    def number(self, name):
        last = Turn(LB, NB - 1, NB - 1)
        return last.number(last_name(last)) + 1 + TAIL_ORDER.index(name)


def last_name(turn):
    return max(turn.order, key=turn.order.get)


PROLOGUE = ["norm_A0", "qk_even_A0", "qk_odd_A0", "v_A0",
            "norm_A1", "qk_even_A1", "qk_odd_A1", "v_A1", "shift_first"]
PROLOGUE_STEPS = len(PROLOGUE)
RECIP_QUAD = {LA: 2, LB: 3}
HIGH_B_QUAD = 9
REST_DMAS = 11
CASTS = 5
LOOP_A = (2, 6)
LOOP_B = (2, 7)


def turns(eng, body):
    for layer, (lo, hi) in ((LA, LOOP_A), (LB, LOOP_B)):
        for t in range(lo):
            body(Turn(layer, t, t))
        with eng.Fori(lo, hi) as t:
            body(Turn(layer, t, lo))
        for t in range(hi, NB):
            body(Turn(layer, t, t))


def not_met(count):
    return not isinstance(count, int) or count > 0


def hybrid_block_kernel(nc, x, w_qkv_a, b_qk_a, b_v_a, w_out_a, b_out_a, w_qkv_b, w_out_b,
                        w_gate, w_up, w_down, ident, mask_s, mask_t, rope_cos, rope_sin, out):
    ctx = ExitStack()
    with ctx:
        def sb(name, shape, dt=F32):
            return ctx.enter_context(nc.sbuf_tensor(name, shape, dt))

        def pb(name, shape):
            return ctx.enter_context(nc.psum_tensor(name, shape, F32))

        def sem(name):
            return ctx.enter_context(nc.semaphore(name))

        parts_dram = [nc.dram_tensor(f"parts_{n}", (NB, 2, PARTS, 2, HALF * H, T), BF16).ap() for n in "ab"]
        recip_dram = nc.dram_tensor("recip", (H, T), F32).ap()

        x_all = sb("x_all", [128, NB, TT, D])
        v_all = sb("v_all", [128, NB, TT, D])
        qr = sb("qr", [128, G, J, T], BF16)
        kr = sb("kr", [128, G, J, T], BF16)
        vaug = sb("vaug", [128, G, TT, J, OROW])
        probs = sb("probs", [128, 2, J, T])
        negmax = sb("negmax", [128, 2, J, TT])
        shift_rest = sb("shift_rest", [16, 128])
        shift_parts = sb("shift_parts", [16, PARTS, 128], BF16)
        o_raw = sb("o_raw", [128, 2, T])
        o_cols = sb("o_cols", [128, T])
        sums = sb("sums", [128, T // 8])
        recips = sb("recips", [128, T // 8])
        recip_cols = sb("recip_cols", [128, T])
        attn_t = sb("attn_t", [128, T])
        kinds = ("A", "B", "mid")
        stats = {k: sb(f"stats_{k}", [128, TT, 6]) for k in kinds}
        meanvar = {k: sb(f"meanvar_{k}", [128, TT, 2]) for k in kinds}
        var_eps = {k: sb(f"var_eps_{k}", [128, TT]) for k in kinds}
        rstd = {k: sb(f"rstd_{k}", [128, TT, 1]) for k in kinds}
        centred = {k: sb(f"centred_{k}", [128, TT, D]) for k in kinds}
        normed = {k: sb(f"normed_{k}", [128, TT, D]) for k in kinds}
        normed_t = {k: sb(f"normed_t_{k}", [128, T]) for k in kinds}
        qk_parts = {k: sb(f"qk_parts_{k}", [128, PARTS, 2, T], BF16) for k in "AB"}
        qk_rest = {k: sb(f"qk_rest_{k}", [128, 2, T]) for k in "AB"}
        qk_raw = sb("qk_raw", [128, 2, T])
        by_cos = sb("by_cos", [128, 2, T])
        by_sin = sb("by_sin", [128, 2, T])
        qk_rot = sb("qk_rot", [128, 2, T])
        tanh_g = sb("tanh_g", [128, T])
        gate_act = sb("gate_act", [128, T])
        hidden = sb("hidden", [128, HB, T])
        wqkv = {"A": sb("wqkv_a", [128, 3, D]), "B": sb("wqkv_b", [128, 3, D])}
        wout = [sb("wout_a", [128, D]), sb("wout_b", [128, D])]
        bqk = sb("bqk", [128, 2])
        bv = sb("bv", [128, D])
        bout = sb("bout", [128, D])
        w_int = [sb(f"w_int{n}", [128, HB * 128], I32) for n in range(3)]
        wg = sb("wg", [128, HB * 128])
        wu = sb("wu", [128, HB * 128])
        wd = sb("wd", [128, HB * 128])
        identf = sb("identf", [128, 128])
        masks_f = sb("masks_f", [128, 2, 128])
        identb = sb("identb", [128, 128], BF16)
        masks_b = sb("masks_b", [128, 2, 128], BF16)
        cosines = sb("cosines", [128, T])
        sines = sb("sines", [128, T])
        minus_half = sb("minus_half", [128, TT])
        wait_here = sb("wait_here", [128, 2])

        ps_t = [pb(f"ps_t{n}", [128, T]) for n in range(2)]
        ps_s = [pb(f"ps_s{n}", [128, 2, T]) for n in range(2)]
        ps_o = pb("ps_o", [128, T])
        ps_step = pb("ps_step", [128, T])

        x_first, x_others = sem("x_first"), sem("x_others")
        loaded = {n: sem(f"loaded_{n}") for n in ("ident", "qkv_a", "rest")}
        q_zeroed = sem("q_zeroed")
        k_filled = sem("k_filled")
        vaug_filled = sem("vaug_filled")
        half_filled = sem("half_filled")
        cast = sem("cast")
        step_written = sem("step_written")
        step_read = sem("step_read")
        st_ready = sem("st_ready")
        exp_done = sem("exp_done")
        pv_done = sem("pv_done")
        s_ready = sem("s_ready")
        max_done = sem("max_done")
        rows_loaded = [sem(f"rows_loaded{g}") for g in range(G)]
        vaug_copied = sem("vaug_copied")
        shift_high, shift_mid = sem("shift_high"), sem("shift_mid")
        shift_low = sem("shift_low")
        shift_loaded = sem("shift_loaded")
        o_copied = sem("o_copied")
        o_moved = [sem(f"o_moved{n}") for n in range(2)]
        recip_done = sem("recip_done")
        recip_stored, recip_loaded = sem("recip_stored"), sem("recip_loaded")
        attn_scaled = sem("attn_scaled")
        ln_stats = {k: sem(f"ln_stats_{k}") for k in kinds}
        ln_aggr = {k: sem(f"ln_aggr_{k}") for k in kinds}
        ln_eps = {k: sem(f"ln_eps_{k}") for k in kinds}
        ln_rstd = {k: sem(f"ln_rstd_{k}") for k in kinds}
        ln_done = {k: sem(f"ln_done_{k}") for k in kinds}
        bias_added = sem("bias_added")
        high_done = {k: sem(f"high_done_{k}") for k in "AB"}
        mid_done = {k: sem(f"mid_done_{k}") for k in "AB"}
        rest_done = sem("rest_done_B")
        low_done = {k: sem(f"low_done_{k}") for k in "AB"}
        rope_mul, rope_done = sem("rope_mul"), sem("rope_done")
        parts_stored = [sem("parts_stored_a"), sem("parts_stored_b")]
        tanh_done = sem("tanh_done")
        out_stored = sem("out_stored")

        ROWS_DMAS, SHIFT_DMAS, O_DMAS, PARTS_DMAS = 6, PARTS, 2 * J, 2

        def first_query(layer, kb):
            return kb * 128 if layer == LB else 0

        def last_key(layer, qt):
            return (qt + 1) * 128 if layer == LB else T

        block = ctx.enter_context(nc.Block())

        @block.sync
        def _(sp):
            x_v = x.rearrange("b (i p) d -> p b i d", p=128)
            out_v = out.rearrange("b (i p) d -> p b i d", p=128)

            sp.dma_start(x_all[:, 0, :, :], x_v[:, 0, :, :]).then_inc(x_first, 16)
            sp.dma_start(identf[:, :], ident).then_inc(loaded["ident"], 16)
            sp.dma_start(wqkv["A"][:, :, :], w_qkv_a).then_inc(loaded["qkv_a"], 16)
            sp.dma_start(bqk[:, :], b_qk_a).then_inc(loaded["qkv_a"], 16)
            sp.dma_start(bv[:, :], b_v_a.partition_broadcast(128)).then_inc(loaded["qkv_a"], 16)
            rest = [(bout[:, :], b_out_a.partition_broadcast(128)), (wout[LA][:, :], w_out_a),
                    (wqkv["B"][:, :, :], w_qkv_b), (wout[LB][:, :], w_out_b),
                    (w_int[0][:, :], w_gate), (w_int[1][:, :], w_up), (w_int[2][:, :], w_down),
                    (masks_f[:, 0, :], mask_s), (masks_f[:, 1, :], mask_t),
                    (cosines[:, :], rope_cos), (sines[:, :], rope_sin)]
            assert len(rest) == REST_DMAS
            for b in range(1, NB):
                sp.dma_start(x_all[:, b, :, :], x_v[:, b, :, :]).then_inc(x_others, 16)
            for dst, src in rest:
                sp.dma_start(dst, src).then_inc(loaded["rest"], 16)

            def store_parts(layer, b):
                kind = "AB"[layer]
                sp.wait_ge(low_done[kind], b + 1)
                for side in range(2):
                    sp.dma_start(parts_dram[layer][b, side].rearrange("s e p t -> p (s e) t"),
                                 qk_parts[kind][64 * side:64 * side + 64, :, :, :]
                                 .rearrange("p s e t -> p (s e) t")).then_inc(parts_stored[layer], 16)

            def load_rows(group, number):
                layer, b, g = group
                if not_met(QUADS * (number - G + 1)):
                    sp.wait_ge(st_ready, QUADS * (number - G + 1))
                if g == 0:
                    sp.wait_ge(parts_stored[layer], 16 * PARTS_DMAS * (b + 1))
                heads = slice(J * g, J * g + J)
                q, k = (parts_dram[layer][b, side].rearrange("s e (i h) t -> (s e i) h t", i=HALF)
                        for side in range(2))
                row = 0
                for part, count in ((0, 3), (1, 2), (2, 1)):
                    rows = count * DH
                    sp.dma_start(qr[row:row + rows, g, :, :], q[0:rows, heads, :]).then_inc(rows_loaded[g], 16)
                    k_part = k[DH * part:DH * part + DH, heads, :].unsqueeze(0)
                    sp.dma_start(kr[row:row + rows, g, :, :],
                                 k_part.broadcast_to([count, DH, J, T])).then_inc(rows_loaded[g], 16)
                    row += rows

            def load_shift(g, number):
                sp.wait_ge(shift_low, number + 1)
                for part in range(PARTS):
                    sp.dma_start(qr[SH + part:SH + part + 1, g, :, :],
                                 shift_parts[:, part, :]).then_inc(shift_loaded, 16)

            def move_o(g, number, job):
                sp.wait_ge(o_copied, number + 1)
                if g == 0:
                    if not_met(job):
                        sp.wait_ge(attn_scaled, job)
                for j in range(J):
                    h = J * g + j
                    src = o_raw[OROW * j:OROW * j + DH, g % 2, :]
                    sp.dma_start(o_cols[DH * h:DH * h + DH, :], src).then_inc(o_moved[g % 2], 16)
                    src = o_raw[OROW * j + SUMROW:OROW * j + SUMROW + 1, g % 2, :]
                    sp.dma_start(sums[8 * h:8 * h + 8, :], src).then_inc(o_moved[g % 2], 16)

            def spread_recips(job):
                sp.wait_ge(recip_done, job + 1)
                sp.dma_start(recip_dram.rearrange("h (c t) -> (h c) t", c=8), recips[:, :]).then_inc(recip_stored, 16)
                sp.wait_ge(recip_stored, 16 * (job + 1))
                src = recip_dram.unsqueeze(1).broadcast_to([H, DH, T])
                sp.dma_start(recip_cols[:, :], src).then_inc(recip_loaded, 16)

            def store_out(b, down):
                sp.wait_ge(step_read, down + 1)
                sp.dma_start(out_v[:, b, :, :], x_all[:, b, :, :]).then_inc(out_stored, 16)

            def body(turn):
                first = G * turn.job
                for g in range(G):
                    group = turn.group_after(g, 3)
                    if group:
                        load_rows(group, first + g + 3)
                    if turn.job0 or g:
                        move_o((g - 1) % G, first + g - 1, turn.job - (g == 0))
                    if g == 0 and turn.tail:
                        spread_recips(turn.job - 1)
                    group = turn.group_after(g, 1)
                    if group:
                        load_shift(group[2], first + g + 1)
                    if g == 1 and turn.front_a:
                        store_parts(LA, turn.b_a)
                    if g == 3 and turn.front_b:
                        store_parts(LB, turn.b_b)
                if turn.tail and turn.tail_layer == LB:
                    store_out(turn.tail_b, turn.number("down"))

            store_parts(LA, 0)
            for g in range(3):
                if g == 0:
                    sp.wait_ge(q_zeroed, 1)
                    sp.wait_ge(k_filled, 2)
                load_rows((LA, 0, g), g)
            store_parts(LA, 1)
            load_shift(0, 0)
            turns(sp, body)
            move_o(G - 1, G * JOBS - 1, JOBS - 1)
            spread_recips(JOBS - 1)
            store_out(NB - 1, LastTail().number("down"))
            sp.wait_ge(out_stored, 16 * NB)

        @block.tensor
        def _(pe):
            def step_bank(number):
                if not_met(number):
                    pe.wait_ge(step_read, number)

            def transpose_norm(kind, count, number):
                step_bank(number)
                pe.wait_ge(ln_done[kind], count)
                for i in range(TT):
                    mm = nc.tensor.transpose(ps_step[:, 128 * i:128 * i + 128], normed[kind][:, i, :], identf[:, :])
                mm.then_inc(step_written, 1)

            def project_qk(kind, e, number):
                step_bank(number)
                nc.tensor.matmul(ps_step[:, :], wqkv[kind][:, e, :], normed_t[kind][:, :],
                                 start=True, stop=True).then_inc(step_written, 1)

            def project_v(kind, number):
                step_bank(number)
                for i in range(TT):
                    mm = nc.tensor.matmul(ps_step[:, 128 * i:128 * i + 128],
                                          normed_t[kind][:, 128 * i:128 * i + 128], wqkv[kind][:, 2, :],
                                          start=True, stop=True)
                mm.then_inc(step_written, 1)

            def transpose_max(parity, number_of_group, number):
                step_bank(number)
                pe.wait_ge(max_done, 2 * TT * (number_of_group + 1))
                src = negmax[:, parity, :, :].rearrange("p j q -> p (j q)")
                nc.tensor.transpose(ps_step[0:16, 0:128], src, identf[:, :]).then_inc(step_written, 1)

            def out_proj(turn, number):
                step_bank(number)
                pe.wait_ge(attn_scaled, turn.job)
                for i in range(TT):
                    mm = nc.tensor.matmul(ps_step[:, 128 * i:128 * i + 128], attn_t[:, 128 * i:128 * i + 128],
                                          wout[turn.tail_layer][:, :], start=True, stop=True)
                mm.then_inc(step_written, 1)

            def project_hidden(w, hb, number):
                step_bank(number)
                nc.tensor.matmul(ps_step[:, :], w[:, 128 * hb:128 * hb + 128], normed_t["mid"][:, :],
                                 start=True, stop=True).then_inc(step_written, 1)

            def down_proj(number):
                step_bank(number)
                for i in range(TT):
                    for hb in range(HB):
                        mm = nc.tensor.matmul(ps_step[:, 128 * i:128 * i + 128],
                                              hidden[:, hb, 128 * i:128 * i + 128], wd[:, 128 * hb:128 * hb + 128],
                                              start=hb == 0, stop=hb == HB - 1)
                mm.then_inc(step_written, 1)

            def step(turn, u, half):
                name = turn.steps.get((u, half))
                if name is None:
                    return
                number = turn.number(name)
                if name == "norm_A":
                    transpose_norm("A", turn.b_a + 1, number)
                elif name == "norm_B":
                    transpose_norm("B", turn.b_b + 1, number)
                elif name == "norm_mid":
                    transpose_norm("mid", turn.job, number)
                elif name == "qk_even_A":
                    project_qk("A", 0, number)
                elif name == "qk_odd_A":
                    project_qk("A", 1, number)
                elif name == "qk_even_B":
                    project_qk("B", 0, number)
                elif name == "qk_odd_B":
                    project_qk("B", 1, number)
                elif name == "v_A":
                    project_v("A", number)
                elif name == "v_B":
                    project_v("B", number)
                elif name == "out_proj":
                    out_proj(turn, number)
                elif name == "down":
                    down_proj(number)
                elif name.startswith("gate"):
                    project_hidden(wg, int(name[-1]), number)
                elif name.startswith("up"):
                    project_hidden(wu, int(name[-1]), number)
                elif name.startswith("shift"):
                    g = int(name[-1])
                    transpose_max((g + 1) % 2, G * turn.job + g + 1, number)

            def scores(layer, g, qt, pair, number_of_group, job):
                number = 2 * TT * number_of_group + 2 * qt + pair
                if qt == 0 and pair == 0:
                    pe.wait_ge(rows_loaded[g], 16 * ROWS_DMAS * (job + 1))
                if not_met(number - 1):
                    pe.wait_ge(max_done, number - 1)
                bank = ps_s[pair]
                keys = last_key(layer, qt)
                for n in range(2):
                    j = 2 * pair + n
                    mm = nc.tensor.matmul(bank[:, n, 0:keys], qr[0:SH, g, j, 128 * qt:128 * qt + 128],
                                          kr[0:SH, g, j, 0:keys], start=True, stop=layer == LA)
                    if layer == LB:
                        mm = nc.tensor.matmul(bank[:, n, keys - 128:keys], identb[:, :], masks_b[:, 0, :],
                                              start=False, stop=True)
                mm.then_inc(s_ready, 1)

            def scores_t(layer, g, kb, j, number):
                if not_met(number - 1):
                    pe.wait_ge(exp_done, number - 1)
                q0 = first_query(layer, kb)
                bank = ps_t[j % 2]
                mm = nc.tensor.matmul(bank[:, q0:T], kr[0:KROWS, g, j, 128 * kb:128 * kb + 128],
                                      qr[0:KROWS, g, j, q0:T], start=True, stop=layer == LA)
                if layer == LB:
                    mm = nc.tensor.matmul(bank[:, q0:q0 + 128], identb[:, :], masks_b[:, 1, :],
                                          start=False, stop=True)
                mm.then_inc(st_ready, 1)

            def weigh_values(layer, g, kb, quad, number_of_group):
                if kb == 0:
                    if not_met(number_of_group):
                        pe.wait_ge(o_copied, number_of_group)
                    pe.wait_ge(vaug_copied, number_of_group + 1)
                pe.wait_ge(exp_done, J * (quad + 1))
                q0 = first_query(layer, kb)
                for j in range(J):
                    mm = nc.tensor.matmul(ps_o[OROW * j:OROW * j + OROW, q0:T], vaug[:, g, kb, j, :],
                                          probs[:, kb % 2, j, q0:T], start=kb == 0, stop=kb == TT - 1)
                mm.then_inc(pv_done, 1)

            def body(turn):
                for u in range(QUADS):
                    g, kb = divmod(u, TT)
                    quad = QUADS * turn.job + u
                    group = turn.group_after(g, 2)
                    if kb == 0:
                        pe.wait_ge(shift_loaded, 16 * SHIFT_DMAS * (G * turn.job + g + 1))
                    ahead = G * turn.job + g + 2
                    scores_t(turn.layer, g, kb, 0, J * quad)
                    scores_t(turn.layer, g, kb, 1, J * quad + 1)
                    if group:
                        scores(group[0], group[2], kb, 0, ahead, turn.job + (g >= 2))
                    step(turn, u, 0)
                    scores_t(turn.layer, g, kb, 2, J * quad + 2)
                    if group:
                        scores(group[0], group[2], kb, 1, ahead, turn.job + (g >= 2))
                    scores_t(turn.layer, g, kb, 3, J * quad + 3)
                    step(turn, u, 1)
                    if turn.job0 or u:
                        before = (u - 1) % QUADS
                        weigh_values(turn.layer if u else turn.tail_layer, before // TT, before % TT,
                                     quad - 1, G * turn.job + g - (kb == 0))

            pe.wait_ge(loaded["ident"], 16)
            transpose_norm("A", 1, 0)
            pe.wait_ge(loaded["qkv_a"], 48)
            project_qk("A", 0, 1)
            project_qk("A", 1, 2)
            project_v("A", 3)
            for qt in range(TT):
                for pair in range(2):
                    scores(LA, 0, qt, pair, 0, 0)
                if qt == 0:
                    transpose_norm("A", 2, 4)
                elif qt == 1:
                    project_qk("A", 0, 5)
                elif qt == 2:
                    project_qk("A", 1, 6)
                else:
                    project_v("A", 7)
            for qt in range(TT):
                for pair in range(2):
                    scores(LA, 1, qt, pair, 1, 0)
                if qt == 0:
                    transpose_max(0, 0, 8)
            pe.wait_ge(cast, CASTS)
            pe.wait_ge(loaded["rest"], 16 * REST_DMAS)
            turns(pe, body)
            weigh_values(LB, G - 1, TT - 1, QUADS * JOBS - 1, G * JOBS - 1)
            last = LastTail()
            for name in TAIL_ORDER:
                number = last.number(name)
                if name == "out_proj":
                    out_proj(last, number)
                elif name == "norm_mid":
                    transpose_norm("mid", JOBS, number)
                elif name == "down":
                    down_proj(number)
                else:
                    project_hidden(wg if name[0] == "g" else wu, int(name[-1]), number)

        @block.scalar
        def _(act):
            def copy_norm(kind, number):
                act.wait_ge(step_written, number + 1)
                nc.scalar.copy(normed_t[kind][:, :], ps_step[:, :]).then_inc(step_read, 1)

            def high_part_a(e, b, number):
                act.wait_ge(step_written, number + 1)
                if not_met(16 * PARTS_DMAS * b):
                    act.wait_ge(parts_stored[LA], 16 * PARTS_DMAS * b)
                nc.scalar.activation(qk_parts["A"][:, 0, e, :], ps_step[:, :], ACT.Identity,
                                     bias=bqk[:, e:e + 1]).then_inc(high_done["A"], 1)

            def mid_part(kind, b, odd=None):
                if kind == "A":
                    act.wait_ge(step_read, odd + 1)
                else:
                    act.wait_ge(rest_done, b + 1)
                nc.scalar.copy(qk_parts[kind][:, 1, :, :], qk_rest[kind][:, :, :]).then_inc(mid_done[kind], 1)

            def raw_b(e, b, number):
                act.wait_ge(step_written, number + 1)
                act.wait_ge(rope_mul, 2 * b)
                nc.scalar.copy(qk_raw[:, e, :], ps_step[:, :]).then_inc(step_read, 1)

            def high_part_b(b):
                act.wait_ge(rope_done, 2 * (b + 1))
                act.wait_ge(parts_stored[LB], 16 * PARTS_DMAS * b)
                nc.scalar.copy(qk_parts["B"][:, 0, :, :], qk_rot[:, :, :]).then_inc(high_done["B"], 1)

            def shift_high_part(number_of_group, number):
                act.wait_ge(step_written, number + 1)
                if not_met(16 * SHIFT_DMAS * number_of_group):
                    act.wait_ge(shift_loaded, 16 * SHIFT_DMAS * number_of_group)
                nc.scalar.copy(shift_parts[:, 0, :], ps_step[0:16, 0:128]).then_inc(shift_high, 1)

            def shift_mid_part(number):
                act.wait_ge(step_read, number + 1)
                nc.scalar.copy(shift_parts[:, 1, :], shift_rest[:, :]).then_inc(shift_mid, 1)

            def tanh(job, hb, number):
                act.wait_ge(step_written, number + 1)
                nc.scalar.activation(tanh_g[:, :], ps_step[:, :], ACT.Tanh, scale=0.5).then_inc(tanh_done, 1)

            def copy_o(g, job):
                act.wait_ge(pv_done, TT * (G * job + g + 1))
                if not_met(16 * O_DMAS * (2 * job + g // 2)):
                    act.wait_ge(o_moved[g % 2], 16 * O_DMAS * (2 * job + g // 2))
                nc.scalar.copy(o_raw[:, g % 2, :], ps_o[:, :]).then_inc(o_copied, 1)

            def exp(layer, kb, j, quad):
                unit = J * quad + j
                q0 = first_query(layer, kb)
                act.wait_ge(st_ready, unit + 1)
                if j == 0:
                    if not_met(quad - 1):
                        act.wait_ge(pv_done, quad - 1)
                nc.scalar.activation(probs[:, kb % 2, j, q0:T], ps_t[j % 2][:, q0:T], ACT.Exp,
                                     scale=1.0 if layer == LA else float(DH) ** -0.5).then_inc(exp_done, 1)

            def step(turn, u, half):
                name = turn.steps.get((u, half))
                if name is not None:
                    number = turn.number(name)
                    if name == "norm_A":
                        copy_norm("A", number)
                    elif name == "norm_B":
                        copy_norm("B", number)
                    elif name == "norm_mid":
                        copy_norm("mid", number)
                    elif name == "qk_even_A":
                        high_part_a(0, turn.b_a, number)
                    elif name == "qk_odd_A":
                        high_part_a(1, turn.b_a, number)
                    elif name == "qk_even_B":
                        raw_b(0, turn.b_b, number)
                    elif name == "qk_odd_B":
                        raw_b(1, turn.b_b, number)
                    elif name.startswith("gate"):
                        tanh(turn.job - 1, int(name[-1]), number)
                    elif name.startswith("shift"):
                        shift_high_part(G * turn.job + int(name[-1]) + 1, number)

            def body(turn):
                for u in range(QUADS):
                    g, kb = divmod(u, TT)
                    quad = QUADS * turn.job + u
                    exp(turn.layer, kb, 0, quad)
                    exp(turn.layer, kb, 1, quad)
                    if kb == 1 and (turn.job0 or g):
                        copy_o((g - 1) % G, turn.job - (g == 0))
                    step(turn, u, 0)
                    exp(turn.layer, kb, 2, quad)
                    exp(turn.layer, kb, 3, quad)
                    if kb == 1 and turn.group_after(g, 1):
                        shift_mid_part(turn.number(f"shift{g}"))
                    if u == 3 and turn.front_a:
                        mid_part("A", turn.b_a, turn.number("qk_odd_A"))
                    if u == HIGH_B_QUAD and turn.front_b:
                        high_part_b(turn.b_b)
                    if u == HIGH_B_QUAD + 2 and turn.front_b:
                        mid_part("B", turn.b_b)
                    step(turn, u, 1)

            act.wait_ge(loaded["qkv_a"], 48)
            for b in range(2):
                copy_norm("A", 4 * b)
                high_part_a(0, b, 4 * b + 1)
                high_part_a(1, b, 4 * b + 2)
                mid_part("A", b, 4 * b + 2)
            shift_high_part(0, 8)
            shift_mid_part(8)
            turns(act, body)
            copy_o(G - 1, JOBS - 1)
            last = LastTail()
            copy_norm("mid", last.number("norm_mid"))
            for hb in range(HB):
                tanh(JOBS - 1, hb, last.number(f"gate{hb}"))

        @block.vector
        def _(dve):
            def norm_stats(kind, b, count):
                nc.vector.memset(wait_here[:, 0:1], 0.0)
                for i in range(TT):
                    op = nc.vector.bn_stats(stats[kind][:, i, :], x_all[:, b, i, :])
                op.then_inc(ln_stats[kind], 1)
                dve.wait_ge(ln_stats[kind], count)
                nc.vector.memset(wait_here[:, 1:2], 0.0)
                for i in range(TT):
                    op = nc.vector.bn_aggr(meanvar[kind][:, i, :], stats[kind][:, i, :])
                op.then_inc(ln_aggr[kind], 1)
                dve.wait_ge(ln_aggr[kind], count)
                nc.vector.tensor_scalar_add(var_eps[kind][:, :], meanvar[kind][:, :, 1], EPS).then_inc(ln_eps[kind], 1)

            def rest_part_a(e, b):
                dve.wait_ge(high_done["A"], 2 * b + e + 1)
                if not_met(b):
                    dve.wait_ge(low_done["A"], b)
                nc.vector.scalar_tensor_tensor(out=qk_rest["A"][:, e, :], in0=ps_step[:, :], scalar=bqk[:, e:e + 1],
                                               in1=qk_parts["A"][:, 0, e, :], op0=ALU.add,
                                               op1=ALU.subtract).then_inc(step_read, 1)

            def copy_v(layer, b, number):
                dve.wait_ge(step_written, number + 1)
                dst = v_all[:, b, :, :]
                src = ps_step[:, :].rearrange("p (i d) -> p i d", i=TT)
                if layer == LA:
                    op = nc.vector.tensor_tensor(dst, src, bv[:, :].unsqueeze(1).broadcast_to([128, TT, D]), ALU.add)
                else:
                    dve.wait_ge(vaug_copied, G * (b + 1))
                    op = nc.vector.tensor_copy(dst, src)
                op.then_inc(step_read, 1)

            def shift_rest_part(number_of_group):
                dve.wait_ge(shift_high, number_of_group + 1)
                nc.vector.tensor_tensor(shift_rest[:, :], ps_step[0:16, 0:128], shift_parts[:, 0, :],
                                        ALU.subtract).then_inc(step_read, 1)

            def shift_low_part(number_of_group):
                dve.wait_ge(shift_mid, number_of_group + 1)
                nc.vector.tensor_tensor(shift_parts[:, 2, :], shift_rest[:, :], shift_parts[:, 1, :],
                                        ALU.subtract).then_inc(shift_low, 1)

            def residual(b, number):
                dve.wait_ge(step_written, number + 1)
                nc.vector.tensor_tensor(x_all[:, b, :, :], ps_step[:, :].rearrange("p (i d) -> p i d", i=TT),
                                        x_all[:, b, :, :], ALU.add).then_inc(step_read, 1)
                dve.wait_ge(step_read, number + 1)

            def gate(job, hb):
                count = HB * job + hb + 1
                dve.wait_ge(tanh_done, count)
                nc.vector.scalar_tensor_tensor(out=gate_act[:, :], in0=tanh_g[:, :], scalar=1.0, in1=ps_step[:, :],
                                               op0=ALU.add, op1=ALU.mult).then_inc(step_read, 1)

            def up(hb, number):
                dve.wait_ge(step_written, number + 1)
                nc.vector.tensor_tensor(hidden[:, hb, :], ps_step[:, :], gate_act[:, :], ALU.mult).then_inc(step_read, 1)

            def reciprocals(job):
                for half in range(2):
                    dve.wait_ge(o_moved[half], 16 * O_DMAS * (G // 2) * (job + 1))
                nc.vector.reciprocal(recips[:, :], sums[:, :]).then_inc(recip_done, 1)

            def maxima(layer, g, qt, pair, number):
                keys = last_key(layer, qt)
                dve.wait_ge(s_ready, number + 1)
                nc.vector.tensor_reduce(negmax[:, g % 2, 2 * pair:2 * pair + 2, qt], ps_s[pair][:, :, 0:keys],
                                        AX.X, ALU.max, negate=True).then_inc(max_done, 1)

            def step(turn, u, half):
                name = turn.steps.get((u, half))
                if name is not None:
                    number = turn.number(name)
                    if name == "qk_even_A":
                        rest_part_a(0, turn.b_a)
                    elif name == "qk_odd_A":
                        rest_part_a(1, turn.b_a)
                    elif name == "v_A":
                        copy_v(LA, turn.b_a, number)
                    elif name == "v_B":
                        copy_v(LB, turn.b_b, number)
                    elif name == "out_proj":
                        residual(turn.tail_b, number)
                        norm_stats("mid", turn.tail_b, turn.job)
                    elif name == "down":
                        residual(turn.tail_b, number)
                    elif name.startswith("gate"):
                        gate(turn.job - 1, int(name[-1]))
                    elif name.startswith("up"):
                        up(int(name[-1]), number)
                    elif name.startswith("shift"):
                        shift_rest_part(G * turn.job + int(name[-1]) + 1)

            def body(turn):
                for u in range(QUADS):
                    g, kb = divmod(u, TT)
                    group = turn.group_after(g, 2)
                    pairs = 2 * (QUADS * turn.job + u + 2 * TT)
                    if u == 0 and turn.front_a:
                        norm_stats("A", turn.b_a, turn.b_a + 1)
                    if group:
                        maxima(group[0], group[2], kb, 0, pairs)
                    step(turn, u, 0)
                    if u == 0 and turn.front_b:
                        norm_stats("B", turn.b_b, turn.b_b + 1)
                    if u == RECIP_QUAD[turn.layer] and turn.tail:
                        reciprocals(turn.job - 1)
                    if group:
                        maxima(group[0], group[2], kb, 1, pairs + 1)
                    if kb == 1 and turn.group_after(g, 1):
                        shift_low_part(G * turn.job + g + 1)
                    step(turn, u, 1)

            nc.vector.memset(qr[:, :, :, :].rearrange("p g j t -> p (g j t)").bitcast(F32), 0.0).then_inc(q_zeroed, 1)
            dve.wait_ge(x_first, 16)
            norm_stats("A", 0, 1)
            dve.wait_ge(loaded["qkv_a"], 48)
            rest_part_a(0, 0)
            rest_part_a(1, 0)
            copy_v(LA, 0, 3)
            dve.wait_ge(x_others, 16 * (NB - 1))
            norm_stats("A", 1, 2)
            dve.wait_ge(loaded["rest"], 16 * REST_DMAS)
            for dst, src, scale in ((wg, w_int[0], 1.0 / 127.0), (wu, w_int[1], 1.0 / 127.0), (wd, w_int[2], 0.5 / 127.0)):
                nc.vector.tensor_scalar(dst[:, :], src[:, :], scale, None, ALU.mult).then_inc(cast, 1)
            nc.vector.tensor_copy(identb[:, :], identf[:, :]).then_inc(cast, 1)
            nc.vector.tensor_copy(masks_b[:, :, :], masks_f[:, :, :]).then_inc(cast, 1)
            for g in range(2):
                for qt in range(TT):
                    for pair in range(2):
                        maxima(LA, g, qt, pair, 2 * TT * g + 2 * qt + pair)
                    if g == 0:
                        if qt == 1:
                            rest_part_a(0, 1)
                        elif qt == 2:
                            rest_part_a(1, 1)
                        elif qt == 3:
                            copy_v(LA, 1, 7)
                    elif qt == 0:
                        shift_rest_part(0)
                    elif qt == 1:
                        shift_low_part(0)
            turns(dve, body)
            reciprocals(JOBS - 1)
            last = LastTail()
            residual(NB - 1, last.number("out_proj"))
            norm_stats("mid", NB - 1, JOBS)
            for hb in range(HB):
                gate(JOBS - 1, hb)
                up(hb, last.number(f"up{hb}"))
            residual(NB - 1, last.number("down"))

        @block.gpsimd
        def _(pool):
            def norm(kind, b, count):
                pool.wait_ge(ln_eps[kind], count)
                nc.gpsimd.tensor_tensor(rstd[kind][:, :, 0], var_eps[kind][:, :], minus_half[:, :],
                                        ALU.pow).then_inc(ln_rstd[kind], 1)
                mean = meanvar[kind][:, :, 0:1].broadcast_to([128, TT, D])
                nc.gpsimd.tensor_tensor(centred[kind][:, :, :], x_all[:, b, :, :], mean,
                                        ALU.subtract).then_inc(ln_rstd[kind], 1)
                pool.wait_ge(ln_rstd[kind], 2 * count)
                nc.gpsimd.tensor_tensor(normed[kind][:, :, :], centred[kind][:, :, :],
                                        rstd[kind][:, :, :].broadcast_to([128, TT, D]),
                                        ALU.mult).then_inc(ln_done[kind], 1)

            def add_bias(b):
                nc.gpsimd.tensor_tensor(x_all[:, b, :, :], x_all[:, b, :, :],
                                        bout[:, :].unsqueeze(1).broadcast_to([128, TT, D]),
                                        ALU.add).then_inc(bias_added, 1)

            def copy_values(group, number):
                layer, b, g = group
                if not_met(TT * (number - G + 1)):
                    pool.wait_ge(pv_done, TT * (number - G + 1))
                src = v_all[:, b, :, J * DH * g:J * DH * (g + 1)].rearrange("p i (j d) -> p i j d", j=J)
                nc.gpsimd.tensor_copy(vaug[:, g, :, :, 0:DH], src).then_inc(vaug_copied, 1)

            def low_part(kind, b):
                pool.wait_ge(mid_done[kind], b + 1)
                nc.gpsimd.tensor_tensor(qk_parts[kind][:, 2, :, :], qk_rest[kind][:, :, :], qk_parts[kind][:, 1, :, :],
                                        ALU.subtract).then_inc(low_done[kind], 1)

            def rope(b, odd):
                pool.wait_ge(step_read, odd + 1)
                both = [128, 2, T]
                nc.gpsimd.tensor_tensor(by_cos[:, :, :], qk_raw[:, :, :], cosines[:, :].unsqueeze(1).broadcast_to(both),
                                        ALU.mult).then_inc(rope_mul, 1)
                nc.gpsimd.tensor_tensor(by_sin[:, :, :], qk_raw[:, :, :], sines[:, :].unsqueeze(1).broadcast_to(both),
                                        ALU.mult).then_inc(rope_mul, 1)
                pool.wait_ge(rope_mul, 2 * (b + 1))
                nc.gpsimd.tensor_tensor(qk_rot[:, 0, :], by_cos[:, 0, :], by_sin[:, 1, :],
                                        ALU.subtract).then_inc(rope_done, 1)
                nc.gpsimd.tensor_tensor(qk_rot[:, 1, :], by_sin[:, 0, :], by_cos[:, 1, :],
                                        ALU.add).then_inc(rope_done, 1)

            def rest_part_b(b):
                pool.wait_ge(high_done["B"], b + 1)
                nc.gpsimd.tensor_tensor(qk_rest["B"][:, :, :], qk_rot[:, :, :], qk_parts["B"][:, 0, :, :],
                                        ALU.subtract).then_inc(rest_done, 1)

            def scale_attn(job):
                pool.wait_ge(recip_loaded, 16 * (job + 1))
                nc.gpsimd.tensor_tensor(attn_t[:, :], o_cols[:, :], recip_cols[:, :], ALU.mult).then_inc(attn_scaled, 1)

            def body(turn):
                first = G * turn.job
                if turn.front_a:
                    norm("A", turn.b_a, turn.b_a + 1)
                    add_bias(turn.b_a)
                for g in range(G):
                    group = turn.group_after(g, 3)
                    if group:
                        copy_values(group, first + g + 3)
                    if g == 0:
                        if turn.front_b:
                            norm("B", turn.b_b, turn.b_b + 1)
                        if turn.tail:
                            scale_attn(turn.job - 1)
                        if turn.front_a:
                            low_part("A", turn.b_a)
                            pool.wait_ge(step_read, turn.number("v_A") + 1)
                    elif g == 1:
                        if turn.tail and turn.layer == LA:
                            norm("mid", turn.tail_b, turn.job)
                        if turn.front_b:
                            rope(turn.b_b, turn.number("qk_odd_B"))
                        if turn.tail and turn.layer == LB:
                            norm("mid", turn.tail_b, turn.job)
                    elif g == 2:
                        if turn.front_b:
                            rest_part_b(turn.b_b)
                            low_part("B", turn.b_b)
                            pool.wait_ge(step_read, turn.number("v_B") + 1)

            nc.gpsimd.memset(minus_half[:, :], -0.5).then_inc(half_filled, 1)
            nc.gpsimd.memset(kr[:, :, :, :].rearrange("p g j t -> p (g j t)").bitcast(F32), 0.0).then_inc(k_filled, 1)
            pool.wait_ge(k_filled, 1)
            nc.gpsimd.memset(kr[SH:128, :, :, :], 1.0).then_inc(k_filled, 1)
            pool.wait_ge(k_filled, 2)
            norm("A", 0, 1)
            low_part("A", 0)
            nc.gpsimd.memset(vaug[:, :, :, :, :], 0.0).then_inc(vaug_filled, 1)
            pool.wait_ge(vaug_filled, 1)
            nc.gpsimd.memset(vaug[:, :, :, :, SUMROW:SUMROW + 1], 1.0).then_inc(vaug_filled, 1)
            pool.wait_ge(vaug_filled, 2)
            pool.wait_ge(step_read, 4)
            norm("A", 1, 2)
            for g in range(3):
                copy_values((LA, 0, g), g)
            low_part("A", 1)
            pool.wait_ge(step_read, 8)
            pool.wait_ge(loaded["rest"], 16 * REST_DMAS)
            add_bias(0)
            add_bias(1)
            turns(pool, body)
            scale_attn(JOBS - 1)
            norm("mid", NB - 1, JOBS)


_NAMES = ["x", "w_qkv_a", "b_qk_a", "b_v_a", "w_out_a", "b_out_a", "w_qkv_b", "w_out_b",
          "w_gate", "w_up", "w_down", "ident", "mask_s", "mask_t", "rope_cos", "rope_sin"]


def _by_pairs(w):
    return w.reshape(w.shape[0], H, HALF, 2).transpose(0, 3, 2, 1).reshape(w.shape[0], 2, HALF * H)


def _qkv(wq, wk, wv):
    q, k = _by_pairs(wq), _by_pairs(wk)
    return np.ascontiguousarray(np.stack([np.concatenate([q[:, 0], k[:, 0]], 1),
                                          np.concatenate([q[:, 1], k[:, 1]], 1), wv], 1))


def _rope_tables():
    powers = np.arange(0, DH, 2, dtype=np.float32) / np.float32(DH)
    freqs = (np.float32(1.0) / np.float32(10000.0) ** powers).astype(np.float32)
    angles = np.outer(np.arange(T, dtype=np.float32), freqs).T[None, :, None, :]
    rows = np.broadcast_to(angles, (2, HALF, H, T)).reshape(128, T)
    return np.cos(rows).astype(np.float32), np.sin(rows).astype(np.float32)


def kernel(L0_attn_a_x, L0_attn_a_w1, L0_attn_a_b1, L0_attn_a_w2, L0_attn_a_b2, L0_attn_b_wq, L0_attn_b_wk,
           L0_attn_b_wv, L0_attn_b_wo, L0_ffn_w_gate, L0_ffn_w_up, L0_ffn_w_down):
    import concourse.bacc as _bacc
    from concourse.bass_utils import run_bass_kernel_spmd as _run

    w1, b1 = np.asarray(L0_attn_a_w1), np.asarray(L0_attn_a_b1)
    bq, bk = _by_pairs(b1[None, 0:D])[0], _by_pairs(b1[None, D:2 * D])[0]
    wd = np.asarray(L0_ffn_w_down)
    cos, sin = _rope_tables()
    later = np.arange(128)[None, :] > np.arange(128)[:, None]
    mask_s = np.where(later, np.float32(BIG), np.float32(0.0))
    arrays = dict(
        x=np.asarray(L0_attn_a_x),
        w_qkv_a=_qkv(w1[:, 0:D], w1[:, D:2 * D], w1[:, 2 * D:3 * D]),
        b_qk_a=np.concatenate([bq, bk], 1).T,
        b_v_a=b1[2 * D:3 * D],
        w_out_a=np.asarray(L0_attn_a_w2),
        b_out_a=np.asarray(L0_attn_a_b2),
        w_qkv_b=_qkv(np.asarray(L0_attn_b_wq).T, np.asarray(L0_attn_b_wk).T, np.asarray(L0_attn_b_wv).T),
        w_out_b=np.asarray(L0_attn_b_wo).T,
        w_gate=np.asarray(L0_ffn_w_gate).T,
        w_up=np.asarray(L0_ffn_w_up).T,
        w_down=wd.T.reshape(HB, 128, D).transpose(1, 0, 2).reshape(128, HB * D),
        ident=np.eye(128, dtype=np.float32),
        mask_s=mask_s, mask_t=mask_s.T, rope_cos=cos, rope_sin=sin)
    nc = _bacc.Bacc("TRN2", target_bir_lowering=False, num_devices=1)
    ins, args = {}, []
    for name in _NAMES:
        a = np.ascontiguousarray(arrays[name])
        ins[f"in_{name}"] = a
        args.append(nc.dram_tensor(f"in_{name}", a.shape, mybir.dt.from_np(a.dtype), kind="ExternalInput").ap())
    out = nc.dram_tensor("out_x", (NB, T, D), F32, kind="ExternalOutput").ap()
    hybrid_block_kernel(nc, *args, out)
    r = _run(nc, [ins], core_ids=[0])
    return r.results[0]["out_x"]
```

```python
from contextlib import ExitStack

import numpy as np
import concourse.bass as bass
from concourse import mybir

F32 = mybir.dt.float32
BF16 = mybir.dt.bfloat16
I32 = mybir.dt.int32
ACT = mybir.ActivationFunctionType
ALU = mybir.AluOpType
AX = mybir.AxisListType

NB, T, D, H = 8, 512, 128, 16
DH = D // H
HB = 3
TT = T // 128
G, J = 4, 4
QUADS = G * TT
EPS = 1e-5
PARTS = 3
HALF = DH // 2
PROD = 6 * DH
SH = 96
KROWS = SH + PARTS
BIG = -3.0e38
LA, LB = 0, 1
JOBS = 2 * NB
OROW = 32
SUMROW = DH

FRONT_A = {(1, 1): "norm_A", (2, 1): "qk_even_A", (3, 1): "qk_odd_A", (4, 0): "v_A"}
FRONT_B = {(5, 1): "norm_B", (6, 1): "qk_even_B", (7, 1): "qk_odd_B", (8, 1): "v_B"}
SHIFTS = {(1, 0): "shift0", (5, 0): "shift1", (9, 0): "shift2", (13, 0): "shift3"}
TAIL_IN_A = {(4, 1): "out_proj", (7, 0): "norm_mid", (8, 0): "gate0", (9, 1): "up0", (10, 1): "gate1",
             (11, 1): "up1", (12, 1): "gate2", (13, 1): "up2", (14, 1): "down"}
TAIL_IN_B = {(7, 0): "out_proj", (10, 0): "norm_mid", (10, 1): "gate0", (11, 1): "up0", (12, 0): "gate1",
             (12, 1): "up1", (13, 1): "gate2", (14, 1): "up2", (15, 1): "down"}
TAIL_ORDER = ["out_proj", "norm_mid", "gate0", "up0", "gate1", "up1", "gate2", "up2", "down"]


class Turn:

    def __init__(self, layer, t, t0):
        self.layer, self.t, self.t0 = layer, t, t0
        self.job, self.job0 = layer * NB + t, layer * NB + t0
        self.front_a = layer == LA and t0 + 2 < NB
        self.tail = self.job0 > 0
        self.front_b = 2 <= self.job0 < NB + 2
        self.b_a = t + 2
        self.b_b = self.job - 2
        prev = self.job - 1
        self.tail_layer = LA if self.job0 <= NB else LB
        self.tail_b = prev - self.tail_layer * NB
        steps = dict(SHIFTS)
        if self.job0 == JOBS - 1:
            del steps[(13, 0)]
        if self.front_a:
            steps.update(FRONT_A)
        if self.tail:
            steps.update(TAIL_IN_A if layer == LA else TAIL_IN_B)
        if self.front_b:
            steps.update(FRONT_B)
        self.steps = steps
        self.order = {name: i for i, (_, name) in enumerate(sorted(steps.items()))}

    def number(self, name):
        base = PROLOGUE_STEPS
        for job in range(self.job0):
            base += len(Turn(job // NB, job % NB, job % NB).order)
        return base + self.order[name] + len(self.order) * (self.t - self.t0)

    def group_after(self, g, ahead):
        if g + ahead < G:
            return self.layer, self.t, g + ahead
        if self.job0 == JOBS - 1:
            return None
        if self.layer == LA and self.t0 == NB - 1:
            return LB, 0, g + ahead - G
        return self.layer, self.t + 1, g + ahead - G


class LastTail:
    job, tail_layer, tail_b = JOBS, LB, NB - 1

    def number(self, name):
        last = Turn(LB, NB - 1, NB - 1)
        return last.number(last_name(last)) + 1 + TAIL_ORDER.index(name)


def last_name(turn):
    return max(turn.order, key=turn.order.get)


PROLOGUE = ["norm_A0", "qk_even_A0", "qk_odd_A0", "v_A0",
            "norm_A1", "shift_first", "qk_even_A1", "qk_odd_A1", "v_A1"]
PROLOGUE_STEPS = len(PROLOGUE)
RECIP_QUAD = {LA: 2, LB: 3}
HIGH_B_QUAD = 11
REST_DMAS = 11
CASTS = 5
TWO_ONES = float(np.array([0x3F803F80], np.uint32).view(np.float32)[0])
LOOP_A = (2, 6)
LOOP_B = (2, 7)


def turns(eng, body):
    for layer, (lo, hi) in ((LA, LOOP_A), (LB, LOOP_B)):
        for t in range(lo):
            body(Turn(layer, t, t))
        with eng.Fori(lo, hi) as t:
            body(Turn(layer, t, lo))
        for t in range(hi, NB):
            body(Turn(layer, t, t))


def not_met(count):
    return not isinstance(count, int) or count > 0


def hybrid_block_kernel(nc, x, w_qkv_a, b_qk_a, b_v_a, w_out_a, b_out_a, w_qkv_b, w_out_b,
                        w_gate, w_up, w_down, ident, mask_s, mask_t, rope_cos, rope_sin, out):
    ctx = ExitStack()
    with ctx:
        def sb(name, shape, dt=F32):
            return ctx.enter_context(nc.sbuf_tensor(name, shape, dt))

        def pb(name, shape):
            return ctx.enter_context(nc.psum_tensor(name, shape, F32))

        def sem(name):
            return ctx.enter_context(nc.semaphore(name))

        parts_dram = [nc.dram_tensor(f"parts_{n}", (NB, 2, PARTS, 2, HALF * H, T), BF16).ap() for n in "ab"]
        recip_dram = nc.dram_tensor("recip", (H, T), F32).ap()

        x_all = sb("x_all", [128, NB, TT, D])
        v_all = sb("v_all", [128, NB, TT, D])
        qr = sb("qr", [128, G, J, T], BF16)
        kr = sb("kr", [128, G, J, T], BF16)
        vaug = sb("vaug", [128, G, TT, J, OROW])
        probs = sb("probs", [128, 2, J, T])
        negmax = sb("negmax", [128, J, TT])
        negmax_rest = sb("negmax_rest", [128, J, TT])
        negmax_cols = sb("negmax_cols", [128, 128], BF16)
        negmax_parts = negmax_cols[:, 0:PARTS * J * TT].rearrange("p (s j q) -> p s j q", s=PARTS, j=J)
        shift_rows = sb("shift_rows", [PARTS * J * TT, 128], BF16)
        o_raw = sb("o_raw", [128, 2, T])
        o_cols = sb("o_cols", [128, T])
        sums = sb("sums", [128, T // 8])
        recips = sb("recips", [128, T // 8])
        recip_cols = sb("recip_cols", [128, T])
        attn_t = sb("attn_t", [128, T])
        kinds = ("A", "B", "mid")
        stats = {k: sb(f"stats_{k}", [128, TT, 6]) for k in kinds}
        meanvar = {k: sb(f"meanvar_{k}", [128, TT, 2]) for k in kinds}
        var_eps = {k: sb(f"var_eps_{k}", [128, TT]) for k in kinds}
        rstd = {k: sb(f"rstd_{k}", [128, TT, 1]) for k in kinds}
        centred = {k: sb(f"centred_{k}", [128, TT, D]) for k in kinds}
        normed = {k: sb(f"normed_{k}", [128, TT, D]) for k in kinds}
        normed_t = {k: sb(f"normed_t_{k}", [128, T]) for k in kinds}
        qk_parts = {k: sb(f"qk_parts_{k}", [128, PARTS, 2, T], BF16) for k in "AB"}
        qk_rest = {k: sb(f"qk_rest_{k}", [128, 2, T]) for k in "AB"}
        qk_raw = sb("qk_raw", [128, 2, T])
        by_cos = sb("by_cos", [128, 2, T])
        by_sin = sb("by_sin", [128, 2, T])
        qk_rot = sb("qk_rot", [128, 2, T])
        tanh_g = sb("tanh_g", [128, T])
        gate_act = sb("gate_act", [128, T])
        hidden = sb("hidden", [128, HB, T])
        wqkv = {"A": sb("wqkv_a", [128, 3, D]), "B": sb("wqkv_b", [128, 3, D])}
        wout = [sb("wout_a", [128, D]), sb("wout_b", [128, D])]
        bqk = sb("bqk", [128, 2])
        bv = sb("bv", [128, D])
        bout = sb("bout", [128, D])
        w_int = [sb(f"w_int{n}", [128, HB * 128], I32) for n in range(3)]
        wg = sb("wg", [128, HB * 128])
        wu = sb("wu", [128, HB * 128])
        wd = sb("wd", [128, HB * 128])
        identf = sb("identf", [128, 128])
        masks_f = sb("masks_f", [128, 2, 128])
        identb = sb("identb", [128, 128], BF16)
        masks_b = sb("masks_b", [128, 2, 128], BF16)
        cosines = sb("cosines", [128, T])
        sines = sb("sines", [128, T])
        minus_half = sb("minus_half", [128, TT])
        wait_here = sb("wait_here", [128, 2])

        ps_t = [pb(f"ps_t{n}", [128, T]) for n in range(2)]
        ps_s = [pb(f"ps_s{n}", [128, 2, T]) for n in range(2)]
        ps_o = pb("ps_o", [128, T])
        ps_step = pb("ps_step", [128, T])
        ps_step_b = ps_step[:, :].bitcast(BF16)

        x_first, x_others = sem("x_first"), sem("x_others")
        loaded = {n: sem(f"loaded_{n}") for n in ("ident", "qkv_a", "rest")}
        q_zeroed = sem("q_zeroed")
        k_filled = sem("k_filled")
        vaug_filled = sem("vaug_filled")
        half_filled = sem("half_filled")
        cast = sem("cast")
        step_written = sem("step_written")
        step_read = sem("step_read")
        st_ready = sem("st_ready")
        exp_done = sem("exp_done")
        pv_done = sem("pv_done")
        s_ready = sem("s_ready")
        max_done = sem("max_done")
        rows_loaded = [sem(f"rows_loaded{g}") for g in range(G)]
        vaug_copied = sem("vaug_copied")
        shift_split = sem("shift_split")
        shift_loaded = sem("shift_loaded")
        o_copied = sem("o_copied")
        o_moved = [sem(f"o_moved{n}") for n in range(2)]
        recip_done = sem("recip_done")
        recip_stored, recip_loaded = sem("recip_stored"), sem("recip_loaded")
        attn_scaled = sem("attn_scaled")
        ln_stats = {k: sem(f"ln_stats_{k}") for k in kinds}
        ln_aggr = {k: sem(f"ln_aggr_{k}") for k in kinds}
        ln_eps = {k: sem(f"ln_eps_{k}") for k in kinds}
        ln_rstd = {k: sem(f"ln_rstd_{k}") for k in kinds}
        ln_done = {k: sem(f"ln_done_{k}") for k in kinds}
        bias_added = sem("bias_added")
        high_done = {k: sem(f"high_done_{k}") for k in "AB"}
        mid_done = {k: sem(f"mid_done_{k}") for k in "AB"}
        rest_done = sem("rest_done_B")
        low_done = {k: sem(f"low_done_{k}") for k in "AB"}
        rope_mul, rope_done = sem("rope_mul"), sem("rope_done")
        parts_stored = [sem("parts_stored_a"), sem("parts_stored_b")]
        tanh_done = sem("tanh_done")
        out_stored = sem("out_stored")

        ROWS_DMAS, O_DMAS, PARTS_DMAS = 6, J + 1, 2

        def first_query(layer, kb):
            return kb * 128 if layer == LB else 0

        def last_key(layer, qt):
            return (qt + 1) * 128 if layer == LB else T

        block = ctx.enter_context(nc.Block())

        @block.sync
        def _(sp):
            x_v = x.rearrange("b (i p) d -> p b i d", p=128)
            out_v = out.rearrange("b (i p) d -> p b i d", p=128)

            sp.dma_start(x_all[:, 0, :, :], x_v[:, 0, :, :]).then_inc(x_first, 16)
            sp.dma_start(identf[:, :], ident).then_inc(loaded["ident"], 16)
            sp.dma_start(wqkv["A"][:, :, :], w_qkv_a).then_inc(loaded["qkv_a"], 16)
            sp.dma_start(bqk[:, :], b_qk_a).then_inc(loaded["qkv_a"], 16)
            sp.dma_start(bv[:, :], b_v_a.partition_broadcast(128)).then_inc(loaded["qkv_a"], 16)
            rest = [(bout[:, :], b_out_a.partition_broadcast(128)), (wout[LA][:, :], w_out_a),
                    (wqkv["B"][:, :, :], w_qkv_b), (wout[LB][:, :], w_out_b),
                    (w_int[0][:, :], w_gate), (w_int[1][:, :], w_up), (w_int[2][:, :], w_down),
                    (masks_f[:, 0, :], mask_s), (masks_f[:, 1, :], mask_t),
                    (cosines[:, :], rope_cos), (sines[:, :], rope_sin)]
            assert len(rest) == REST_DMAS
            sp.dma_start(x_all[:, 1:NB, :, :].rearrange("p b i d -> p (b i) d"),
                         x_v[:, 1:NB, :, :].rearrange("p b i d -> p (b i) d")).then_inc(x_others, 16)

            def store_parts(layer, b):
                kind = "AB"[layer]
                sp.wait_ge(low_done[kind], b + 1)
                for side in range(2):
                    sp.dma_start(parts_dram[layer][b, side].rearrange("s e p t -> p (s e) t"),
                                 qk_parts[kind][64 * side:64 * side + 64, :, :, :]
                                 .rearrange("p s e t -> p (s e) t")).then_inc(parts_stored[layer], 16)

            def load_rows(group, number):
                layer, b, g = group
                if not_met(QUADS * (number - G + 1)):
                    sp.wait_ge(st_ready, QUADS * (number - G + 1))
                if g == 0:
                    sp.wait_ge(parts_stored[layer], 16 * PARTS_DMAS * (b + 1))
                heads = slice(J * g, J * g + J)
                q, k = (parts_dram[layer][b, side].rearrange("s e (i h) t -> (s e i) h t", i=HALF)
                        for side in range(2))
                row = 0
                for part, count in ((0, 3), (1, 2), (2, 1)):
                    rows = count * DH
                    sp.dma_start(qr[row:row + rows, g, :, :], q[0:rows, heads, :]).then_inc(rows_loaded[g], 16)
                    k_part = k[DH * part:DH * part + DH, heads, :].unsqueeze(0)
                    sp.dma_start(kr[row:row + rows, g, :, :],
                                 k_part.broadcast_to([count, DH, J, T])).then_inc(rows_loaded[g], 16)
                    row += rows

            def load_shift(g, number):
                sp.wait_ge(step_read, number + 1)
                sp.dma_start(qr[SH:KROWS, g, :, :], shift_rows[:, :]).then_inc(shift_loaded, 16)

            def move_o(g, number, job):
                sp.wait_ge(o_copied, number + 1)
                if g == 0:
                    if not_met(job):
                        sp.wait_ge(attn_scaled, job)
                for j in range(J):
                    h = J * g + j
                    src = o_raw[OROW * j:OROW * j + DH, g % 2, :]
                    sp.dma_start(o_cols[DH * h:DH * h + DH, :], src).then_inc(o_moved[g % 2], 16)
                src = o_raw[SUMROW:128:OROW, g % 2, :]
                sp.dma_start(sums[8 * J * g:8 * J * (g + 1), :], src).then_inc(o_moved[g % 2], 16)

            def spread_recips(job):
                sp.wait_ge(recip_done, job + 1)
                sp.dma_start(recip_dram.rearrange("h (c t) -> (h c) t", c=8), recips[:, :]).then_inc(recip_stored, 16)
                sp.wait_ge(recip_stored, 16 * (job + 1))
                src = recip_dram.unsqueeze(1).broadcast_to([H, DH, T])
                sp.dma_start(recip_cols[:, :], src).then_inc(recip_loaded, 16)

            def store_out(b, down):
                sp.wait_ge(step_read, down + 1)
                sp.dma_start(out_v[:, b, :, :], x_all[:, b, :, :]).then_inc(out_stored, 16)

            def body(turn):
                first = G * turn.job
                for g in range(G):
                    group = turn.group_after(g, 3)
                    if group:
                        load_rows(group, first + g + 3)
                    if turn.job0 or g:
                        move_o((g - 1) % G, first + g - 1, turn.job - (g == 0))
                    group = turn.group_after(g, 1)
                    if group:
                        load_shift(group[2], turn.number(f"shift{g}"))
                    if g == 0 and turn.tail:
                        spread_recips(turn.job - 1)
                    if g == 1 and turn.front_a:
                        store_parts(LA, turn.b_a)
                    if g == 3 and turn.front_b:
                        store_parts(LB, turn.b_b)
                if turn.tail and turn.tail_layer == LB:
                    store_out(turn.tail_b, turn.number("down"))

            store_parts(LA, 0)
            for g in range(3):
                if g == 0:
                    sp.wait_ge(q_zeroed, 1)
                    sp.wait_ge(k_filled, 2)
                load_rows((LA, 0, g), g)
            for dst, src in rest:
                sp.dma_start(dst, src).then_inc(loaded["rest"], 16)
            load_shift(0, 5)
            store_parts(LA, 1)
            turns(sp, body)
            move_o(G - 1, G * JOBS - 1, JOBS - 1)
            spread_recips(JOBS - 1)
            store_out(NB - 1, LastTail().number("down"))
            sp.wait_ge(out_stored, 16 * NB)

        @block.tensor
        def _(pe):
            def step_bank(number):
                if not_met(number):
                    pe.wait_ge(step_read, number)

            def transpose_norm(kind, count, number):
                step_bank(number)
                pe.wait_ge(ln_done[kind], count)
                for i in range(TT):
                    mm = nc.tensor.transpose(ps_step[:, 128 * i:128 * i + 128], normed[kind][:, i, :], identf[:, :])
                mm.then_inc(step_written, 1)

            def project_qk(kind, e, number):
                step_bank(number)
                nc.tensor.matmul(ps_step[:, :], wqkv[kind][:, e, :], normed_t[kind][:, :],
                                 start=True, stop=True).then_inc(step_written, 1)

            def project_v(kind, number):
                step_bank(number)
                for i in range(TT):
                    mm = nc.tensor.matmul(ps_step[:, 128 * i:128 * i + 128],
                                          normed_t[kind][:, 128 * i:128 * i + 128], wqkv[kind][:, 2, :],
                                          start=True, stop=True)
                mm.then_inc(step_written, 1)

            def transpose_max(number_of_group, number):
                step_bank(number)
                pe.wait_ge(shift_split, 4 * (number_of_group + 1))
                nc.tensor.transpose(ps_step_b[:, 0:128], negmax_cols[:, :], identb[:, :]).then_inc(step_written, 1)

            def out_proj(turn, number):
                step_bank(number)
                pe.wait_ge(attn_scaled, turn.job)
                for i in range(TT):
                    mm = nc.tensor.matmul(ps_step[:, 128 * i:128 * i + 128], attn_t[:, 128 * i:128 * i + 128],
                                          wout[turn.tail_layer][:, :], start=True, stop=True)
                mm.then_inc(step_written, 1)

            def project_hidden(w, hb, number):
                step_bank(number)
                nc.tensor.matmul(ps_step[:, :], w[:, 128 * hb:128 * hb + 128], normed_t["mid"][:, :],
                                 start=True, stop=True).then_inc(step_written, 1)

            def down_proj(number):
                step_bank(number)
                for i in range(TT):
                    for hb in range(HB):
                        mm = nc.tensor.matmul(ps_step[:, 128 * i:128 * i + 128],
                                              hidden[:, hb, 128 * i:128 * i + 128], wd[:, 128 * hb:128 * hb + 128],
                                              start=hb == 0, stop=hb == HB - 1)
                mm.then_inc(step_written, 1)

            def step(turn, u, half):
                name = turn.steps.get((u, half))
                if name is None:
                    return
                number = turn.number(name)
                if name == "norm_A":
                    transpose_norm("A", turn.b_a + 1, number)
                elif name == "norm_B":
                    transpose_norm("B", turn.b_b + 1, number)
                elif name == "norm_mid":
                    transpose_norm("mid", turn.job, number)
                elif name == "qk_even_A":
                    project_qk("A", 0, number)
                elif name == "qk_odd_A":
                    project_qk("A", 1, number)
                elif name == "qk_even_B":
                    project_qk("B", 0, number)
                elif name == "qk_odd_B":
                    project_qk("B", 1, number)
                elif name == "v_A":
                    project_v("A", number)
                elif name == "v_B":
                    project_v("B", number)
                elif name == "out_proj":
                    out_proj(turn, number)
                elif name == "down":
                    down_proj(number)
                elif name.startswith("gate"):
                    project_hidden(wg, int(name[-1]), number)
                elif name.startswith("up"):
                    project_hidden(wu, int(name[-1]), number)
                elif name.startswith("shift"):
                    g = int(name[-1])
                    transpose_max(G * turn.job + g + 1, number)

            def scores(layer, g, qt, pair, number_of_group, job):
                number = 2 * TT * number_of_group + 2 * qt + pair
                if qt == 0 and pair == 0:
                    pe.wait_ge(rows_loaded[g], 16 * ROWS_DMAS * (job + 1))
                if not_met(number - 1):
                    pe.wait_ge(max_done, number - 1)
                bank = ps_s[pair]
                keys = last_key(layer, qt)
                for n in range(2):
                    j = 2 * pair + n
                    mm = nc.tensor.matmul(bank[:, n, 0:keys], qr[0:SH, g, j, 128 * qt:128 * qt + 128],
                                          kr[0:SH, g, j, 0:keys], start=True, stop=layer == LA)
                    if layer == LB:
                        mm = nc.tensor.matmul(bank[:, n, keys - 128:keys], identb[:, :], masks_b[:, 0, :],
                                              start=False, stop=True)
                mm.then_inc(s_ready, 1)

            def scores_t(layer, g, kb, j, number):
                if not_met(number - 1):
                    pe.wait_ge(exp_done, number - 1)
                q0 = first_query(layer, kb)
                bank = ps_t[j % 2]
                mm = nc.tensor.matmul(bank[:, q0:T], kr[0:KROWS, g, j, 128 * kb:128 * kb + 128],
                                      qr[0:KROWS, g, j, q0:T], start=True, stop=layer == LA)
                if layer == LB:
                    mm = nc.tensor.matmul(bank[:, q0:q0 + 128], identb[:, :], masks_b[:, 1, :],
                                          start=False, stop=True)
                mm.then_inc(st_ready, 1)

            def weigh_values(layer, g, kb, quad, number_of_group):
                if kb == 0:
                    if not_met(number_of_group):
                        pe.wait_ge(o_copied, number_of_group)
                    pe.wait_ge(vaug_copied, number_of_group + 1)
                pe.wait_ge(exp_done, J * (quad + 1))
                q0 = first_query(layer, kb)
                for j in range(J):
                    mm = nc.tensor.matmul(ps_o[OROW * j:OROW * j + OROW, q0:T], vaug[:, g, kb, j, :],
                                          probs[:, kb % 2, j, q0:T], start=kb == 0, stop=kb == TT - 1)
                mm.then_inc(pv_done, 1)

            def body(turn):
                for u in range(QUADS):
                    g, kb = divmod(u, TT)
                    quad = QUADS * turn.job + u
                    group = turn.group_after(g, 2)
                    if kb == 0:
                        pe.wait_ge(shift_loaded, 16 * (G * turn.job + g + 1))
                    ahead = G * turn.job + g + 2
                    scores_t(turn.layer, g, kb, 0, J * quad)
                    scores_t(turn.layer, g, kb, 1, J * quad + 1)
                    if group:
                        scores(group[0], group[2], kb, 0, ahead, turn.job + (g >= 2))
                    step(turn, u, 0)
                    scores_t(turn.layer, g, kb, 2, J * quad + 2)
                    if group:
                        scores(group[0], group[2], kb, 1, ahead, turn.job + (g >= 2))
                    scores_t(turn.layer, g, kb, 3, J * quad + 3)
                    step(turn, u, 1)
                    if turn.job0 or u:
                        before = (u - 1) % QUADS
                        weigh_values(turn.layer if u else turn.tail_layer, before // TT, before % TT,
                                     quad - 1, G * turn.job + g - (kb == 0))

            pe.wait_ge(cast, 1)
            transpose_norm("A", 1, 0)
            pe.wait_ge(loaded["qkv_a"], 48)
            project_qk("A", 0, 1)
            project_qk("A", 1, 2)
            project_v("A", 3)
            for qt in range(TT):
                for pair in range(2):
                    scores(LA, 0, qt, pair, 0, 0)
            transpose_norm("A", 2, 4)
            transpose_max(0, 5)
            for qt in range(TT):
                for pair in range(2):
                    scores(LA, 1, qt, pair, 1, 0)
                if qt == 0:
                    project_qk("A", 0, 6)
                elif qt == 1:
                    project_qk("A", 1, 7)
                elif qt == 2:
                    project_v("A", 8)
            pe.wait_ge(cast, CASTS)
            pe.wait_ge(loaded["rest"], 16 * REST_DMAS)
            turns(pe, body)
            weigh_values(LB, G - 1, TT - 1, QUADS * JOBS - 1, G * JOBS - 1)
            last = LastTail()
            for name in TAIL_ORDER:
                number = last.number(name)
                if name == "out_proj":
                    out_proj(last, number)
                elif name == "norm_mid":
                    transpose_norm("mid", JOBS, number)
                elif name == "down":
                    down_proj(number)
                else:
                    project_hidden(wg if name[0] == "g" else wu, int(name[-1]), number)

        @block.scalar
        def _(act):
            def copy_norm(kind, number):
                act.wait_ge(step_written, number + 1)
                nc.scalar.copy(normed_t[kind][:, :], ps_step[:, :]).then_inc(step_read, 1)

            def high_part_a(e, b, number):
                act.wait_ge(step_written, number + 1)
                if not_met(16 * PARTS_DMAS * b):
                    act.wait_ge(parts_stored[LA], 16 * PARTS_DMAS * b)
                nc.scalar.activation(qk_parts["A"][:, 0, e, :], ps_step[:, :], ACT.Identity,
                                     bias=bqk[:, e:e + 1]).then_inc(high_done["A"], 1)

            def mid_part(kind, b, odd=None):
                if kind == "A":
                    act.wait_ge(step_read, odd + 1)
                else:
                    act.wait_ge(rest_done, b + 1)
                nc.scalar.copy(qk_parts[kind][:, 1, :, :], qk_rest[kind][:, :, :]).then_inc(mid_done[kind], 1)

            def raw_b(e, b, number):
                act.wait_ge(step_written, number + 1)
                act.wait_ge(rope_mul, 2 * b)
                nc.scalar.copy(qk_raw[:, e, :], ps_step[:, :]).then_inc(step_read, 1)

            def high_part_b(b):
                act.wait_ge(rope_done, 2 * (b + 1))
                act.wait_ge(parts_stored[LB], 16 * PARTS_DMAS * b)
                nc.scalar.copy(qk_parts["B"][:, 0, :, :], qk_rot[:, :, :]).then_inc(high_done["B"], 1)

            def copy_shift(number_of_group, number):
                act.wait_ge(step_written, number + 1)
                act.wait_ge(shift_loaded, 16 * number_of_group)
                nc.scalar.copy(shift_rows[:, :], ps_step_b[0:PARTS * J * TT, 0:128]).then_inc(step_read, 1)

            def tanh(job, hb, number):
                act.wait_ge(step_written, number + 1)
                nc.scalar.activation(tanh_g[:, :], ps_step[:, :], ACT.Tanh, scale=0.5).then_inc(tanh_done, 1)

            def copy_o(g, job):
                act.wait_ge(pv_done, TT * (G * job + g + 1))
                if not_met(16 * O_DMAS * (2 * job + g // 2)):
                    act.wait_ge(o_moved[g % 2], 16 * O_DMAS * (2 * job + g // 2))
                nc.scalar.copy(o_raw[:, g % 2, :], ps_o[:, :]).then_inc(o_copied, 1)

            def exp(layer, kb, j, quad):
                unit = J * quad + j
                q0 = first_query(layer, kb)
                act.wait_ge(st_ready, unit + 1)
                if j == 0:
                    if not_met(quad - 1):
                        act.wait_ge(pv_done, quad - 1)
                nc.scalar.activation(probs[:, kb % 2, j, q0:T], ps_t[j % 2][:, q0:T], ACT.Exp,
                                     scale=1.0 if layer == LA else float(DH) ** -0.5).then_inc(exp_done, 1)

            def step(turn, u, half):
                name = turn.steps.get((u, half))
                if name is not None:
                    number = turn.number(name)
                    if name == "norm_A":
                        copy_norm("A", number)
                    elif name == "norm_B":
                        copy_norm("B", number)
                    elif name == "norm_mid":
                        copy_norm("mid", number)
                    elif name == "qk_even_A":
                        high_part_a(0, turn.b_a, number)
                    elif name == "qk_odd_A":
                        high_part_a(1, turn.b_a, number)
                    elif name == "qk_even_B":
                        raw_b(0, turn.b_b, number)
                    elif name == "qk_odd_B":
                        raw_b(1, turn.b_b, number)
                    elif name.startswith("gate"):
                        tanh(turn.job - 1, int(name[-1]), number)
                    elif name.startswith("shift"):
                        copy_shift(G * turn.job + int(name[-1]) + 1, number)

            def body(turn):
                for u in range(QUADS):
                    g, kb = divmod(u, TT)
                    quad = QUADS * turn.job + u
                    exp(turn.layer, kb, 0, quad)
                    exp(turn.layer, kb, 1, quad)
                    if kb == 1 and (turn.job0 or g):
                        copy_o((g - 1) % G, turn.job - (g == 0))
                    step(turn, u, 0)
                    exp(turn.layer, kb, 2, quad)
                    exp(turn.layer, kb, 3, quad)
                    if u == 4 and turn.front_a:
                        mid_part("A", turn.b_a, turn.number("qk_odd_A"))
                    if u == HIGH_B_QUAD and turn.front_b:
                        high_part_b(turn.b_b)
                    if u == HIGH_B_QUAD + 2 and turn.front_b:
                        mid_part("B", turn.b_b)
                    step(turn, u, 1)

            act.wait_ge(loaded["qkv_a"], 48)
            for b, number in enumerate((0, 5)):
                if b == 0:
                    copy_norm("A", 0)
                else:
                    copy_norm("A", 4)
                    copy_shift(0, 5)
                high_part_a(0, b, number + 1)
                high_part_a(1, b, number + 2)
                mid_part("A", b, number + 2)
            turns(act, body)
            copy_o(G - 1, JOBS - 1)
            last = LastTail()
            copy_norm("mid", last.number("norm_mid"))
            for hb in range(HB):
                tanh(JOBS - 1, hb, last.number(f"gate{hb}"))

        @block.vector
        def _(dve):
            def norm_stats(kind, b, count):
                for i in range(TT):
                    op = nc.vector.bn_stats(stats[kind][:, i, :], x_all[:, b, i, :])
                op.then_inc(ln_stats[kind], 1)
                dve.wait_ge(ln_stats[kind], count)
                nc.vector.memset(wait_here[:, 0:1], 0.0)
                for i in range(TT):
                    op = nc.vector.bn_aggr(meanvar[kind][:, i, :], stats[kind][:, i, :])
                op.then_inc(ln_aggr[kind], 1)
                dve.wait_ge(ln_aggr[kind], count)
                nc.vector.tensor_scalar_add(var_eps[kind][:, :], meanvar[kind][:, :, 1], EPS).then_inc(ln_eps[kind], 1)

            def rest_part_a(e, b):
                dve.wait_ge(high_done["A"], 2 * b + e + 1)
                if not_met(b):
                    dve.wait_ge(low_done["A"], b)
                nc.vector.scalar_tensor_tensor(out=qk_rest["A"][:, e, :], in0=ps_step[:, :], scalar=bqk[:, e:e + 1],
                                               in1=qk_parts["A"][:, 0, e, :], op0=ALU.add,
                                               op1=ALU.subtract).then_inc(step_read, 1)

            def copy_v(layer, b, number):
                dve.wait_ge(step_written, number + 1)
                dst = v_all[:, b, :, :]
                src = ps_step[:, :].rearrange("p (i d) -> p i d", i=TT)
                if layer == LA:
                    op = nc.vector.tensor_tensor(dst, src, bv[:, :].unsqueeze(1).broadcast_to([128, TT, D]), ALU.add)
                else:
                    dve.wait_ge(vaug_copied, G * (b + 1))
                    op = nc.vector.tensor_copy(dst, src)
                op.then_inc(step_read, 1)

            def split_maxima(number_of_group):
                before = 4 * number_of_group
                high, mid, low = (negmax_parts[:, n, :, :] for n in range(PARTS))
                dve.wait_ge(max_done, 2 * TT * (number_of_group + 1))
                nc.vector.tensor_copy(high, negmax[:, :, :]).then_inc(shift_split, 1)
                dve.wait_ge(shift_split, before + 1)
                nc.vector.tensor_tensor(negmax_rest[:, :, :], negmax[:, :, :], high, ALU.subtract).then_inc(shift_split, 1)
                dve.wait_ge(shift_split, before + 2)
                nc.vector.tensor_copy(mid, negmax_rest[:, :, :]).then_inc(shift_split, 1)
                dve.wait_ge(shift_split, before + 3)
                nc.vector.tensor_tensor(low, negmax_rest[:, :, :], mid, ALU.subtract).then_inc(shift_split, 1)

            def residual(b, number):
                dve.wait_ge(step_written, number + 1)
                nc.vector.tensor_tensor(x_all[:, b, :, :], ps_step[:, :].rearrange("p (i d) -> p i d", i=TT),
                                        x_all[:, b, :, :], ALU.add).then_inc(step_read, 1)
                dve.wait_ge(x_first, 16)
                dve.wait_ge(step_read, number + 1)

            def gate(job, hb):
                count = HB * job + hb + 1
                dve.wait_ge(tanh_done, count)
                nc.vector.scalar_tensor_tensor(out=gate_act[:, :], in0=tanh_g[:, :], scalar=1.0, in1=ps_step[:, :],
                                               op0=ALU.add, op1=ALU.mult).then_inc(step_read, 1)

            def up(hb, number):
                dve.wait_ge(step_written, number + 1)
                nc.vector.tensor_tensor(hidden[:, hb, :], ps_step[:, :], gate_act[:, :], ALU.mult).then_inc(step_read, 1)

            def reciprocals(job):
                for half in range(2):
                    dve.wait_ge(o_moved[half], 16 * O_DMAS * (G // 2) * (job + 1))
                nc.vector.reciprocal(recips[:, :], sums[:, :]).then_inc(recip_done, 1)

            def maxima(layer, g, qt, pair, number):
                keys = last_key(layer, qt)
                dve.wait_ge(s_ready, number + 1)
                nc.vector.tensor_reduce(negmax[:, 2 * pair:2 * pair + 2, qt], ps_s[pair][:, :, 0:keys],
                                        AX.X, ALU.max, negate=True).then_inc(max_done, 1)

            def step(turn, u, half):
                name = turn.steps.get((u, half))
                if name is not None:
                    number = turn.number(name)
                    if name == "qk_even_A":
                        rest_part_a(0, turn.b_a)
                    elif name == "qk_odd_A":
                        rest_part_a(1, turn.b_a)
                    elif name == "v_A":
                        copy_v(LA, turn.b_a, number)
                    elif name == "v_B":
                        copy_v(LB, turn.b_b, number)
                    elif name == "out_proj":
                        residual(turn.tail_b, number)
                        norm_stats("mid", turn.tail_b, turn.job)
                    elif name == "down":
                        residual(turn.tail_b, number)
                    elif name.startswith("gate"):
                        gate(turn.job - 1, int(name[-1]))
                    elif name.startswith("up"):
                        up(int(name[-1]), number)

            def body(turn):
                for u in range(QUADS):
                    g, kb = divmod(u, TT)
                    group = turn.group_after(g, 2)
                    pairs = 2 * (QUADS * turn.job + u + 2 * TT)
                    if u == 0 and turn.front_a:
                        norm_stats("A", turn.b_a, turn.b_a + 1)
                    if group:
                        maxima(group[0], group[2], kb, 0, pairs)
                    step(turn, u, 0)
                    if u == 2 and turn.front_b:
                        norm_stats("B", turn.b_b, turn.b_b + 1)
                    if u == RECIP_QUAD[turn.layer] and turn.tail:
                        reciprocals(turn.job - 1)
                    if group:
                        maxima(group[0], group[2], kb, 1, pairs + 1)
                        if kb == TT - 1:
                            split_maxima(G * turn.job + g + 2)
                    step(turn, u, 1)

            dve.wait_ge(x_first, 16)
            norm_stats("A", 0, 1)
            nc.vector.memset(negmax_cols[:, :].bitcast(F32), 0.0)
            dve.wait_ge(loaded["ident"], 16)
            nc.vector.tensor_copy(identb[:, :], identf[:, :]).then_inc(cast, 1)
            nc.vector.memset(qr[:, :, :, :].rearrange("p g j t -> p (g j t)").bitcast(F32), 0.0).then_inc(q_zeroed, 1)
            dve.wait_ge(loaded["qkv_a"], 48)
            rest_part_a(0, 0)
            rest_part_a(1, 0)
            copy_v(LA, 0, 3)
            dve.wait_ge(x_others, 16)
            norm_stats("A", 1, 2)
            for g in range(2):
                for qt in range(TT):
                    for pair in range(2):
                        maxima(LA, g, qt, pair, 2 * TT * g + 2 * qt + pair)
                    if g == 1:
                        if qt == 1:
                            rest_part_a(0, 1)
                        elif qt == 2:
                            rest_part_a(1, 1)
                        elif qt == 3:
                            copy_v(LA, 1, 8)
                split_maxima(g)
            dve.wait_ge(loaded["rest"], 16 * REST_DMAS)
            for dst, src, scale in ((wg, w_int[0], 1.0 / 127.0), (wu, w_int[1], 1.0 / 127.0), (wd, w_int[2], 0.5 / 127.0)):
                nc.vector.tensor_scalar(dst[:, :], src[:, :], scale, None, ALU.mult).then_inc(cast, 1)
            nc.vector.tensor_copy(masks_b[:, :, :], masks_f[:, :, :]).then_inc(cast, 1)
            turns(dve, body)
            reciprocals(JOBS - 1)
            last = LastTail()
            residual(NB - 1, last.number("out_proj"))
            norm_stats("mid", NB - 1, JOBS)
            for hb in range(HB):
                gate(JOBS - 1, hb)
                up(hb, last.number(f"up{hb}"))
            residual(NB - 1, last.number("down"))

        @block.gpsimd
        def _(pool):
            def norm_1(kind, b, count):
                pool.wait_ge(ln_eps[kind], count)
                nc.gpsimd.tensor_tensor(rstd[kind][:, :, 0], var_eps[kind][:, :], minus_half[:, :],
                                        ALU.pow).then_inc(ln_rstd[kind], 1)
                mean = meanvar[kind][:, :, 0:1].broadcast_to([128, TT, D])
                nc.gpsimd.tensor_tensor(centred[kind][:, :, :], x_all[:, b, :, :], mean,
                                        ALU.subtract).then_inc(ln_rstd[kind], 1)

            def norm_2(kind, count):
                pool.wait_ge(ln_rstd[kind], 2 * count)
                nc.gpsimd.tensor_tensor(normed[kind][:, :, :], centred[kind][:, :, :],
                                        rstd[kind][:, :, :].broadcast_to([128, TT, D]),
                                        ALU.mult).then_inc(ln_done[kind], 1)

            def norm(kind, b, count):
                norm_1(kind, b, count)
                norm_2(kind, count)

            def add_bias(b):
                nc.gpsimd.tensor_tensor(x_all[:, b, :, :], x_all[:, b, :, :],
                                        bout[:, :].unsqueeze(1).broadcast_to([128, TT, D]),
                                        ALU.add).then_inc(bias_added, 1)

            def copy_values(group, number):
                layer, b, g = group
                if not_met(TT * (number - G + 1)):
                    pool.wait_ge(pv_done, TT * (number - G + 1))
                src = v_all[:, b, :, J * DH * g:J * DH * (g + 1)].rearrange("p i (j d) -> p i j d", j=J)
                nc.gpsimd.tensor_copy(vaug[:, g, :, :, 0:DH], src).then_inc(vaug_copied, 1)

            def low_part(kind, b):
                pool.wait_ge(mid_done[kind], b + 1)
                nc.gpsimd.tensor_tensor(qk_parts[kind][:, 2, :, :], qk_rest[kind][:, :, :], qk_parts[kind][:, 1, :, :],
                                        ALU.subtract).then_inc(low_done[kind], 1)

            def rope_1(b, odd):
                pool.wait_ge(step_read, odd + 1)
                both = [128, 2, T]
                nc.gpsimd.tensor_tensor(by_cos[:, :, :], qk_raw[:, :, :], cosines[:, :].unsqueeze(1).broadcast_to(both),
                                        ALU.mult).then_inc(rope_mul, 1)
                nc.gpsimd.tensor_tensor(by_sin[:, :, :], qk_raw[:, :, :], sines[:, :].unsqueeze(1).broadcast_to(both),
                                        ALU.mult).then_inc(rope_mul, 1)

            def rope_2(b):
                pool.wait_ge(rope_mul, 2 * (b + 1))
                nc.gpsimd.tensor_tensor(qk_rot[:, 0, :], by_cos[:, 0, :], by_sin[:, 1, :],
                                        ALU.subtract).then_inc(rope_done, 1)
                nc.gpsimd.tensor_tensor(qk_rot[:, 1, :], by_sin[:, 0, :], by_cos[:, 1, :],
                                        ALU.add).then_inc(rope_done, 1)

            def rest_part_b(b):
                pool.wait_ge(high_done["B"], b + 1)
                nc.gpsimd.tensor_tensor(qk_rest["B"][:, :, :], qk_rot[:, :, :], qk_parts["B"][:, 0, :, :],
                                        ALU.subtract).then_inc(rest_done, 1)

            def scale_attn(job):
                pool.wait_ge(recip_loaded, 16 * (job + 1))
                nc.gpsimd.tensor_tensor(attn_t[:, :], o_cols[:, :], recip_cols[:, :], ALU.mult).then_inc(attn_scaled, 1)

            def body(turn):
                first = G * turn.job
                late = turn.layer == LB
                if turn.front_a:
                    norm_1("A", turn.b_a, turn.b_a + 1)
                    norm_2("A", turn.b_a + 1)
                    add_bias(turn.b_a)
                for u in range(QUADS):
                    g, kb = divmod(u, TT)
                    group = turn.group_after(g, 3)
                    if kb == 1 and group:
                        copy_values(group, first + g + 3)
                    if turn.front_b:
                        if u == 3:
                            norm_1("B", turn.b_b, turn.b_b + 1)
                        elif u == 4:
                            norm_2("B", turn.b_b + 1)
                        elif u == 8:
                            rope_1(turn.b_b, turn.number("qk_odd_B"))
                        elif u == 9:
                            rope_2(turn.b_b)
                        elif u == 11:
                            rest_part_b(turn.b_b)
                        elif u == 14:
                            low_part("B", turn.b_b)
                            pool.wait_ge(step_read, turn.number("v_B") + 1)
                    if turn.tail:
                        if u == (6 if late else 3):
                            scale_attn(turn.job - 1)
                        elif u == (8 if late else 6):
                            norm_1("mid", turn.tail_b, turn.job)
                        elif u == (9 if late else 7):
                            norm_2("mid", turn.job)
                    if u == 5 and turn.front_a:
                        low_part("A", turn.b_a)
                        pool.wait_ge(step_read, turn.number("v_A") + 1)

            nc.gpsimd.memset(minus_half[:, :], -0.5).then_inc(half_filled, 1)
            pool.wait_ge(half_filled, 1)
            norm("A", 0, 1)
            kr_words = kr[:, :, :, :].rearrange("p g j t -> p (g j t)").bitcast(F32)
            nc.gpsimd.memset(kr_words, 0.0).then_inc(k_filled, 1)
            pool.wait_ge(k_filled, 1)
            nc.gpsimd.memset(kr_words[SH:128, :], TWO_ONES).then_inc(k_filled, 1)
            pool.wait_ge(k_filled, 2)
            low_part("A", 0)
            nc.gpsimd.memset(vaug[:, :, :, :, :], 0.0).then_inc(vaug_filled, 1)
            pool.wait_ge(vaug_filled, 1)
            nc.gpsimd.memset(vaug[:, :, :, :, SUMROW:SUMROW + 1], 1.0).then_inc(vaug_filled, 1)
            pool.wait_ge(vaug_filled, 2)
            pool.wait_ge(step_read, 4)
            norm("A", 1, 2)
            for g in range(3):
                copy_values((LA, 0, g), g)
            low_part("A", 1)
            pool.wait_ge(step_read, 9)
            pool.wait_ge(loaded["rest"], 16 * REST_DMAS)
            add_bias(0)
            add_bias(1)
            turns(pool, body)
            scale_attn(JOBS - 1)
            norm("mid", NB - 1, JOBS)


_NAMES = ["x", "w_qkv_a", "b_qk_a", "b_v_a", "w_out_a", "b_out_a", "w_qkv_b", "w_out_b",
          "w_gate", "w_up", "w_down", "ident", "mask_s", "mask_t", "rope_cos", "rope_sin"]


def _by_pairs(w):
    return w.reshape(w.shape[0], H, HALF, 2).transpose(0, 3, 2, 1).reshape(w.shape[0], 2, HALF * H)


def _qkv(wq, wk, wv):
    q, k = _by_pairs(wq), _by_pairs(wk)
    return np.ascontiguousarray(np.stack([np.concatenate([q[:, 0], k[:, 0]], 1),
                                          np.concatenate([q[:, 1], k[:, 1]], 1), wv], 1))


def _rope_tables():
    powers = np.arange(0, DH, 2, dtype=np.float32) / np.float32(DH)
    freqs = (np.float32(1.0) / np.float32(10000.0) ** powers).astype(np.float32)
    angles = np.outer(np.arange(T, dtype=np.float32), freqs).T[None, :, None, :]
    rows = np.broadcast_to(angles, (2, HALF, H, T)).reshape(128, T)
    return np.cos(rows).astype(np.float32), np.sin(rows).astype(np.float32)


def kernel(L0_attn_a_x, L0_attn_a_w1, L0_attn_a_b1, L0_attn_a_w2, L0_attn_a_b2, L0_attn_b_wq, L0_attn_b_wk,
           L0_attn_b_wv, L0_attn_b_wo, L0_ffn_w_gate, L0_ffn_w_up, L0_ffn_w_down):
    import concourse.bacc as _bacc
    from concourse.bass_utils import run_bass_kernel_spmd as _run

    w1, b1 = np.asarray(L0_attn_a_w1), np.asarray(L0_attn_a_b1)
    bq, bk = _by_pairs(b1[None, 0:D])[0], _by_pairs(b1[None, D:2 * D])[0]
    wd = np.asarray(L0_ffn_w_down)
    cos, sin = _rope_tables()
    later = np.arange(128)[None, :] > np.arange(128)[:, None]
    mask_s = np.where(later, np.float32(BIG), np.float32(0.0))
    arrays = dict(
        x=np.asarray(L0_attn_a_x),
        w_qkv_a=_qkv(w1[:, 0:D], w1[:, D:2 * D], w1[:, 2 * D:3 * D]),
        b_qk_a=np.concatenate([bq, bk], 1).T,
        b_v_a=b1[2 * D:3 * D],
        w_out_a=np.asarray(L0_attn_a_w2),
        b_out_a=np.asarray(L0_attn_a_b2),
        w_qkv_b=_qkv(np.asarray(L0_attn_b_wq).T, np.asarray(L0_attn_b_wk).T, np.asarray(L0_attn_b_wv).T),
        w_out_b=np.asarray(L0_attn_b_wo).T,
        w_gate=np.asarray(L0_ffn_w_gate).T,
        w_up=np.asarray(L0_ffn_w_up).T,
        w_down=wd.T.reshape(HB, 128, D).transpose(1, 0, 2).reshape(128, HB * D),
        ident=np.eye(128, dtype=np.float32),
        mask_s=mask_s, mask_t=mask_s.T, rope_cos=cos, rope_sin=sin)
    nc = _bacc.Bacc("TRN2", target_bir_lowering=False, num_devices=1)
    ins, args = {}, []
    for name in _NAMES:
        a = np.ascontiguousarray(arrays[name])
        ins[f"in_{name}"] = a
        args.append(nc.dram_tensor(f"in_{name}", a.shape, mybir.dt.from_np(a.dtype), kind="ExternalInput").ap())
    out = nc.dram_tensor("out_x", (NB, T, D), F32, kind="ExternalOutput").ap()
    hybrid_block_kernel(nc, *args, out)
    r = _run(nc, [ins], core_ids=[0])
    return r.results[0]["out_x"]
```

```python
from contextlib import ExitStack

import numpy as np
import concourse.bass as bass
from concourse import mybir

F32 = mybir.dt.float32
BF16 = mybir.dt.bfloat16
I32 = mybir.dt.int32
ACT = mybir.ActivationFunctionType
ALU = mybir.AluOpType
AX = mybir.AxisListType

NB, T, D, H = 8, 512, 128, 16
DH = D // H
HB = 3
TT = T // 128
G, J = 4, 4
QUADS = G * TT
EPS = 1e-5
WSCALE = 1.0 / 127.0
PARTS = 3
HALF = DH // 2
SH = 96
KROWS = SH + PARTS
BIG = -3.0e38
LA, LB = 0, 1
JOBS = 2 * NB
OROW = 32
SUMROW = DH

FRONT_A = {(2, 0): "norm_A", (2, 1): "qk_even_A", (3, 1): "qk_odd_A", (4, 1): "v_A"}
FRONT_B_IN_A = {(6, 0): "norm_B", (6, 1): "qk_even_B", (7, 0): "qk_odd_B", (12, 1): "v_B"}
FRONT_B_IN_B = {(5, 1): "norm_B", (6, 1): "qk_even_B", (7, 1): "qk_odd_B", (8, 0): "v_B"}
SHIFTS = {(1, 0): "shift0", (5, 0): "shift1", (9, 0): "shift2", (13, 0): "shift3"}
TAIL_IN_A = {(5, 1): "out_proj", (7, 1): "norm_mid", (8, 0): "gate0", (9, 1): "up0", (10, 1): "gate1",
             (11, 1): "up1", (13, 1): "gate2", (14, 1): "up2", (15, 1): "down"}
TAIL_IN_B = {(6, 0): "out_proj", (8, 1): "norm_mid", (9, 1): "gate0", (10, 1): "up0", (11, 1): "gate1",
             (12, 1): "up1", (13, 1): "gate2", (14, 1): "up2", (15, 1): "down"}
TAIL_IN_LAST = {(6, 0): "out_proj", (8, 1): "norm_mid", (9, 1): "gate0", (11, 0): "up0", (12, 1): "gate1",
                (14, 0): "up1", (QUADS, 0): "gate2", (QUADS + 1, 0): "up2", (QUADS + 2, 0): "down"}
TAIL_ORDER = ["out_proj", "norm_mid", "gate0", "up0", "gate1", "up1", "gate2", "up2", "down"]


class Turn:

    def __init__(self, layer, t, t0):
        self.layer, self.t, self.t0 = layer, t, t0
        self.job, self.job0 = layer * NB + t, layer * NB + t0
        self.front_a = layer == LA and t0 + 2 < NB
        self.tail = self.job0 > 0
        self.front_b = 2 <= self.job0 < NB + 2
        self.b_a = t + 2
        self.b_b = self.job - 2
        prev = self.job - 1
        self.tail_layer = LA if self.job0 <= NB else LB
        self.tail_b = prev - self.tail_layer * NB
        steps = dict(SHIFTS)
        if self.job0 == JOBS - 1:
            del steps[(13, 0)]
        if self.front_a:
            steps.update(FRONT_A)
        if self.job0 == JOBS - 1:
            steps.update(TAIL_IN_LAST)
        elif self.tail:
            steps.update(TAIL_IN_A if layer == LA else TAIL_IN_B)
        if self.front_b:
            steps.update(FRONT_B_IN_A if layer == LA else FRONT_B_IN_B)
        self.steps = steps
        self.order = {name: i for i, (_, name) in enumerate(sorted(steps.items()))}

    def number(self, name):
        base = PROLOGUE_STEPS
        for job in range(self.job0):
            base += len(Turn(job // NB, job % NB, job % NB).order)
        return base + self.order[name] + len(self.order) * (self.t - self.t0)

    def group_after(self, g, ahead):
        if g + ahead < G:
            return self.layer, self.t, g + ahead
        if self.job0 == JOBS - 1:
            return None
        if self.layer == LA and self.t0 == NB - 1:
            return LB, 0, g + ahead - G
        return self.layer, self.t + 1, g + ahead - G


class LastTail:
    job, tail_layer, tail_b = JOBS, LB, NB - 1

    def number(self, name):
        return last_turn().number("down") + 1 + TAIL_ORDER.index(name)


def last_turn():
    return Turn(LB, NB - 1, NB - 1)


PROLOGUE = ["norm_A0", "qk_even_A0", "qk_odd_A0", "v_A0",
            "norm_A1", "qk_even_A1", "qk_odd_A1", "v_A1", "shift_first"]
PROLOGUE_STEPS = len(PROLOGUE)
RECIP_QUAD = {LA: 2, LB: 3}
HIGH_B_QUAD = 11
REST_DMAS = 11
CASTS = 5
TWO_ONES = float(np.array([0x3F803F80], np.uint32).view(np.float32)[0])
LOOP_A = (2, 6)
LOOP_B = (2, 7)


def turns(eng, body):
    for layer, (lo, hi) in ((LA, LOOP_A), (LB, LOOP_B)):
        for t in range(lo):
            body(Turn(layer, t, t))
        with eng.Fori(lo, hi) as t:
            body(Turn(layer, t, lo))
        for t in range(hi, NB):
            body(Turn(layer, t, t))


def not_met(count):
    return not isinstance(count, int) or count > 0


def hybrid_block_kernel(nc, x, w_qkv_a, b_qk_a, b_v_a, w_out_a, b_out_a, w_qkv_b, w_out_b,
                        w_gate, w_up, w_down, ident, mask_s, mask_t, rope_cos, rope_sin, out):
    ctx = ExitStack()
    with ctx:
        def sb(name, shape, dt=F32):
            return ctx.enter_context(nc.sbuf_tensor(name, shape, dt))

        def pb(name, shape):
            return ctx.enter_context(nc.psum_tensor(name, shape, F32))

        def sem(name):
            return ctx.enter_context(nc.semaphore(name))

        parts_dram = [nc.dram_tensor(f"parts_{n}", (NB, 2, PARTS, 2, HALF * H, T), BF16).ap() for n in "ab"]
        recip_dram = nc.dram_tensor("recip", (H, T), F32).ap()

        x_all = sb("x_all", [128, NB, TT, D])
        v_all = sb("v_all", [128, NB, TT, D])
        qr = sb("qr", [128, G, J, T], BF16)
        kr = sb("kr", [128, G, J, T], BF16)
        vaug = sb("vaug", [128, G, TT, J, OROW])
        probs = sb("probs", [128, 2, J, T])
        negmax = sb("negmax", [128, J, TT])
        negmax_rest = sb("negmax_rest", [128, J, TT])
        negmax_cols = sb("negmax_cols", [128, 128], BF16)
        negmax_parts = negmax_cols[:, 0:PARTS * J * TT].rearrange("p (s j q) -> p s j q", s=PARTS, j=J)
        shift_rows = sb("shift_rows", [PARTS * J * TT, 128], BF16)
        o_raw = sb("o_raw", [128, 2, T])
        o_cols = sb("o_cols", [128, T])
        sums = sb("sums", [128, T // 8])
        recips = sb("recips", [128, T // 8])
        recip_cols = sb("recip_cols", [128, T])
        attn_t = sb("attn_t", [128, T])
        kinds = ("A", "B", "mid")
        stats = {k: sb(f"stats_{k}", [128, TT, 6]) for k in kinds}
        meanvar = {k: sb(f"meanvar_{k}", [128, TT, 2]) for k in kinds}
        var_eps = {k: sb(f"var_eps_{k}", [128, TT]) for k in kinds}
        rstd = {k: sb(f"rstd_{k}", [128, TT, 1]) for k in kinds}
        centred = {k: sb(f"centred_{k}", [128, TT, D]) for k in kinds}
        normed = {k: sb(f"normed_{k}", [128, TT, D]) for k in kinds}
        normed_t = {k: sb(f"normed_t_{k}", [128, T]) for k in kinds}
        qk_parts = {k: sb(f"qk_parts_{k}", [128, PARTS, 2, T], BF16) for k in "AB"}
        qk_rest = {k: sb(f"qk_rest_{k}", [128, 2, T]) for k in "AB"}
        qk_raw = sb("qk_raw", [128, 2, T])
        by_cos = sb("by_cos", [128, 2, T])
        by_sin = sb("by_sin", [128, 2, T])
        qk_rot = sb("qk_rot", [128, 2, T])
        tanh_g = sb("tanh_g", [128, T])
        gate_act = sb("gate_act", [128, T])
        hidden = sb("hidden", [128, HB, T])
        wqkv = {"A": sb("wqkv_a", [128, 3, D]), "B": sb("wqkv_b", [128, 3, D])}
        wout = [sb("wout_a", [128, D]), sb("wout_b", [128, D])]
        bqk = sb("bqk", [128, 2])
        bv = sb("bv", [128, D])
        bout = sb("bout", [128, D])
        w_int = [sb(f"w_int{n}", [128, HB * 128], I32) for n in range(3)]
        wg = sb("wg", [128, HB * 128])
        wu = sb("wu", [128, HB * 128])
        wd = sb("wd", [128, HB * 128])
        identf = sb("identf", [128, 128])
        masks_f = sb("masks_f", [128, 2, 128])
        identb = sb("identb", [128, 128], BF16)
        masks_b = sb("masks_b", [128, 2, 128], BF16)
        cosines = sb("cosines", [128, T])
        sines = sb("sines", [128, T])
        minus_half = sb("minus_half", [128, TT])
        exp_of_half = sb("exp_of_half", [128, TT])
        wait_here = sb("wait_here", [128, 2])

        ps_t = [pb(f"ps_t{n}", [128, T]) for n in range(2)]
        ps_s = [pb(f"ps_s{n}", [128, 2, T]) for n in range(2)]
        ps_o = pb("ps_o", [128, T])
        ps_step = pb("ps_step", [128, T])
        ps_step_b = ps_step[:, :].bitcast(BF16)
        even_bank, odd_bank, norm_1_bank = ps_t[0][:, :], ps_t[1][:, :], ps_o[:, :]
        gate_banks = [ps_s[0][:, 0, :], ps_s[0][:, 1, :], ps_t[0][:, :]]
        up_banks = [ps_s[1][:, 0, :], ps_s[1][:, 1, :], ps_t[1][:, :]]

        x_first, x_second, x_others = sem("x_first"), sem("x_second"), sem("x_others")
        loaded = {n: sem(f"loaded_{n}") for n in ("ident", "qkv_a", "rest")}
        q_zeroed = sem("q_zeroed")
        k_filled = sem("k_filled")
        vaug_filled = sem("vaug_filled")
        half_filled = sem("half_filled")
        cast = sem("cast")
        step_written = sem("step_written")
        step_read = sem("step_read")
        st_ready = sem("st_ready")
        exp_done = sem("exp_done")
        pv_done = sem("pv_done")
        s_ready = sem("s_ready")
        max_done = sem("max_done")
        rows_loaded = [sem(f"rows_loaded{g}") for g in range(G)]
        vaug_copied = sem("vaug_copied")
        shift_split = sem("shift_split")
        shift_loaded = sem("shift_loaded")
        o_copied = sem("o_copied")
        o_moved = [sem(f"o_moved{n}") for n in range(2)]
        sums_moved = [sem(f"sums_moved{n}") for n in range(2)]
        recip_done = sem("recip_done")
        recip_stored, recip_loaded = sem("recip_stored"), sem("recip_loaded")
        attn_scaled = sem("attn_scaled")
        ln_stats = {k: sem(f"ln_stats_{k}") for k in kinds}
        ln_aggr = {k: sem(f"ln_aggr_{k}") for k in kinds}
        ln_eps = {k: sem(f"ln_eps_{k}") for k in kinds}
        ln_rstd = {k: sem(f"ln_rstd_{k}") for k in kinds}
        ln_done = {k: sem(f"ln_done_{k}") for k in kinds}
        bias_added = sem("bias_added")
        high_done = {k: sem(f"high_done_{k}") for k in "AB"}
        mid_done = {k: sem(f"mid_done_{k}") for k in "AB"}
        rest_done = sem("rest_done_B")
        low_done = {k: sem(f"low_done_{k}") for k in "AB"}
        rope_mul, rope_done = sem("rope_mul"), sem("rope_done")
        parts_stored = [sem("parts_stored_a"), sem("parts_stored_b")]
        tanh_done = sem("tanh_done")
        out_stored = sem("out_stored")

        ROWS_DMAS, O_DMAS, PARTS_DMAS = 6, J, 2

        def first_query(layer, kb):
            return kb * 128 if layer == LB else 0

        def query_tile(layer, i):
            return TT - 1 - i if layer == LB else i

        def last_key(layer, qt):
            return (qt + 1) * 128 if layer == LB else T

        block = ctx.enter_context(nc.Block())

        @block.sync
        def _(sp):
            x_v = x.rearrange("b (i p) d -> p b i d", p=128)
            out_v = out.rearrange("b (i p) d -> p b i d", p=128)

            sp.dma_start(x_all[:, 0, :, :], x_v[:, 0, :, :]).then_inc(x_first, 16)
            sp.dma_start(identf[:, :], ident).then_inc(loaded["ident"], 16)
            sp.dma_start(wqkv["A"][:, :, :], w_qkv_a).then_inc(loaded["qkv_a"], 16)
            sp.dma_start(bqk[:, :], b_qk_a).then_inc(loaded["qkv_a"], 16)
            sp.dma_start(bv[:, :], b_v_a.partition_broadcast(128)).then_inc(loaded["qkv_a"], 16)
            rest = [(bout[:, :], b_out_a.partition_broadcast(128)), (wout[LA][:, :], w_out_a),
                    (wqkv["B"][:, :, :], w_qkv_b), (wout[LB][:, :], w_out_b),
                    (w_int[0][:, :], w_gate), (w_int[1][:, :], w_up), (w_int[2][:, :], w_down),
                    (masks_f[:, 0, :], mask_s), (masks_f[:, 1, :], mask_t),
                    (cosines[:, :], rope_cos), (sines[:, :], rope_sin)]
            assert len(rest) == REST_DMAS
            sp.dma_start(x_all[:, 1, :, :], x_v[:, 1, :, :]).then_inc(x_second, 16)
            for dst, src in rest:
                sp.dma_start(dst, src).then_inc(loaded["rest"], 16)

            def store_parts(layer, b):
                kind = "AB"[layer]
                sp.wait_ge(low_done[kind], b + 1)
                for side in range(2):
                    sp.dma_start(parts_dram[layer][b, side].rearrange("s e p t -> p (s e) t"),
                                 qk_parts[kind][64 * side:64 * side + 64, :, :, :]
                                 .rearrange("p s e t -> p (s e) t")).then_inc(parts_stored[layer], 16)

            def load_rows(group, number):
                layer, b, g = group
                if not_met(QUADS * (number - G + 1)):
                    sp.wait_ge(st_ready, QUADS * (number - G + 1))
                if g == 0:
                    sp.wait_ge(parts_stored[layer], 16 * PARTS_DMAS * (b + 1))
                heads = slice(J * g, J * g + J)
                q, k = (parts_dram[layer][b, side].rearrange("s e (i h) t -> (s e i) h t", i=HALF)
                        for side in range(2))
                row = 0
                for part, count in ((0, 3), (1, 2), (2, 1)):
                    rows = count * DH
                    sp.dma_start(qr[row:row + rows, g, :, :], q[0:rows, heads, :]).then_inc(rows_loaded[g], 16)
                    k_part = k[DH * part:DH * part + DH, heads, :].unsqueeze(0)
                    sp.dma_start(kr[row:row + rows, g, :, :],
                                 k_part.broadcast_to([count, DH, J, T])).then_inc(rows_loaded[g], 16)
                    row += rows

            def load_shift(g, number):
                sp.wait_ge(step_read, number + 1)
                sp.dma_start(qr[SH:KROWS, g, :, :], shift_rows[:, :]).then_inc(shift_loaded, 16)

            def move_o(g, number, job):
                sp.wait_ge(o_copied, number + 1)
                sp.dma_start(sums[8 * J * g:8 * J * (g + 1), :],
                             o_raw[SUMROW:128:OROW, g % 2, :]).then_inc(sums_moved[g % 2], 16)
                if g == 0:
                    if not_met(job):
                        sp.wait_ge(attn_scaled, job)
                for j in range(J):
                    h = J * g + j
                    src = o_raw[OROW * j:OROW * j + DH, g % 2, :]
                    sp.dma_start(o_cols[DH * h:DH * h + DH, :], src).then_inc(o_moved[g % 2], 16)

            def spread_recips(job):
                sp.wait_ge(recip_done, job + 1)
                sp.dma_start(recip_dram.rearrange("h (c t) -> (h c) t", c=8), recips[:, :]).then_inc(recip_stored, 16)
                sp.wait_ge(recip_stored, 16 * (job + 1))
                src = recip_dram.unsqueeze(1).broadcast_to([H, DH, T])
                sp.dma_start(recip_cols[:, :], src).then_inc(recip_loaded, 16)

            def store_out(b, down):
                sp.wait_ge(step_read, down + 1)
                sp.dma_start(out_v[:, b, :, :], x_all[:, b, :, :]).then_inc(out_stored, 16)

            def body(turn):
                first = G * turn.job
                for g in range(G):
                    group = turn.group_after(g, 3)
                    if group:
                        load_rows(group, first + g + 3)
                    group = turn.group_after(g, 1)
                    if group:
                        load_shift(group[2], turn.number(f"shift{g}"))
                    if turn.job0 or g:
                        move_o((g - 1) % G, first + g - 1, turn.job - (g == 0))
                    if g == 0 and turn.tail:
                        spread_recips(turn.job - 1)
                    if g == 1 and turn.front_a:
                        store_parts(LA, turn.b_a)
                    if g == 3 and turn.front_b:
                        store_parts(LB, turn.b_b)
                if turn.tail and turn.tail_layer == LB and turn.job0 < JOBS - 1:
                    store_out(turn.tail_b, turn.number("down"))

            store_parts(LA, 0)
            for g in range(3):
                if g == 0:
                    sp.wait_ge(q_zeroed, 1)
                    sp.wait_ge(k_filled, 2)
                load_rows((LA, 0, g), g)
                if g == 0:
                    sp.dma_start(x_all[:, 2:NB, :, :].rearrange("p b i d -> p (b i) d"),
                                 x_v[:, 2:NB, :, :].rearrange("p b i d -> p (b i) d")).then_inc(x_others, 16)
            store_parts(LA, 1)
            load_shift(0, PROLOGUE.index("shift_first"))
            turns(sp, body)
            move_o(G - 1, G * JOBS - 1, JOBS - 1)
            spread_recips(JOBS - 1)
            store_out(NB - 2, last_turn().number("down"))
            store_out(NB - 1, LastTail().number("down"))
            sp.wait_ge(out_stored, 16 * NB)

        @block.tensor
        def _(pe):
            def step_bank(number):
                if not_met(number):
                    pe.wait_ge(step_read, number)

            def transpose_norm(kind, count, number, bank=ps_step[:, :]):
                step_bank(number)
                pe.wait_ge(ln_done[kind], count)
                for i in range(TT):
                    mm = nc.tensor.transpose(bank[:, 128 * i:128 * i + 128], normed[kind][:, i, :], identf[:, :])
                mm.then_inc(step_written, 1)

            def project_qk(kind, e, number, bank=ps_step[:, :]):
                step_bank(number)
                nc.tensor.matmul(bank, wqkv[kind][:, e, :], normed_t[kind][:, :],
                                 start=True, stop=True).then_inc(step_written, 1)

            def project_v(kind, number):
                step_bank(number)
                for i in range(TT):
                    mm = nc.tensor.matmul(ps_step[:, 128 * i:128 * i + 128],
                                          normed_t[kind][:, 128 * i:128 * i + 128], wqkv[kind][:, 2, :],
                                          start=True, stop=True)
                mm.then_inc(step_written, 1)

            def transpose_max(number_of_group, number):
                step_bank(number)
                pe.wait_ge(shift_split, 4 * (number_of_group + 1))
                nc.tensor.transpose(ps_step_b[:, 0:128], negmax_cols[:, :], identb[:, :]).then_inc(step_written, 1)

            def out_proj(turn, number):
                step_bank(number)
                pe.wait_ge(attn_scaled, turn.job)
                for i in range(TT):
                    mm = nc.tensor.matmul(ps_step[:, 128 * i:128 * i + 128], attn_t[:, 128 * i:128 * i + 128],
                                          wout[turn.tail_layer][:, :], start=True, stop=True)
                mm.then_inc(step_written, 1)

            def project_hidden(w, hb, number, bank=ps_step[:, :]):
                step_bank(number)
                nc.tensor.matmul(bank, w[:, 128 * hb:128 * hb + 128], normed_t["mid"][:, :],
                                 start=True, stop=True).then_inc(step_written, 1)

            def down_proj(number):
                step_bank(number)
                for i in range(TT):
                    for hb in range(HB):
                        mm = nc.tensor.matmul(ps_step[:, 128 * i:128 * i + 128],
                                              hidden[:, hb, 128 * i:128 * i + 128], wd[:, 128 * hb:128 * hb + 128],
                                              start=hb == 0, stop=hb == HB - 1)
                mm.then_inc(step_written, 1)

            def step(turn, u, half):
                name = turn.steps.get((u, half))
                if name is None:
                    return
                number = turn.number(name)
                if name == "norm_A":
                    transpose_norm("A", turn.b_a + 1, number)
                elif name == "norm_B":
                    transpose_norm("B", turn.b_b + 1, number)
                elif name == "norm_mid":
                    transpose_norm("mid", turn.job, number)
                elif name == "qk_even_A":
                    project_qk("A", 0, number)
                elif name == "qk_odd_A":
                    project_qk("A", 1, number)
                elif name == "qk_even_B":
                    project_qk("B", 0, number)
                elif name == "qk_odd_B":
                    project_qk("B", 1, number)
                elif name == "v_A":
                    project_v("A", number)
                elif name == "v_B":
                    project_v("B", number)
                elif name == "out_proj":
                    out_proj(turn, number)
                elif name == "down":
                    down_proj(number)
                elif name.startswith("gate"):
                    project_hidden(wg, int(name[-1]), number)
                elif name.startswith("up"):
                    project_hidden(wu, int(name[-1]), number)
                elif name.startswith("shift"):
                    g = int(name[-1])
                    transpose_max(G * turn.job + g + 1, number)

            def scores(layer, g, i, pair, number_of_group, job):
                number = 2 * TT * number_of_group + 2 * i + pair
                qt = query_tile(layer, i)
                if i == 0 and pair == 0:
                    pe.wait_ge(rows_loaded[g], 16 * ROWS_DMAS * (job + 1))
                if not_met(number - 1):
                    pe.wait_ge(max_done, number - 1)
                bank = ps_s[pair]
                keys = last_key(layer, qt)
                for n in range(2):
                    j = 2 * pair + n
                    mm = nc.tensor.matmul(bank[:, n, 0:keys], qr[0:SH, g, j, 128 * qt:128 * qt + 128],
                                          kr[0:SH, g, j, 0:keys], start=True, stop=layer == LA)
                    if layer == LB:
                        mm = nc.tensor.matmul(bank[:, n, keys - 128:keys], identb[:, :], masks_b[:, 0, :],
                                              start=False, stop=True)
                mm.then_inc(s_ready, 1)

            def scores_t(layer, g, kb, j, number):
                if not_met(number - 1):
                    pe.wait_ge(exp_done, number - 1)
                q0 = first_query(layer, kb)
                bank = ps_t[j % 2]
                mm = nc.tensor.matmul(bank[:, q0:T], kr[0:KROWS, g, j, 128 * kb:128 * kb + 128],
                                      qr[0:KROWS, g, j, q0:T], start=True, stop=layer == LA)
                if layer == LB:
                    mm = nc.tensor.matmul(bank[:, q0:q0 + 128], identb[:, :], masks_b[:, 1, :],
                                          start=False, stop=True)
                mm.then_inc(st_ready, 1)

            def weigh_values(layer, g, kb, quad, number_of_group):
                if kb == 0:
                    if not_met(number_of_group):
                        pe.wait_ge(o_copied, number_of_group)
                    pe.wait_ge(vaug_copied, number_of_group + 1)
                pe.wait_ge(exp_done, J * (quad + 1))
                q0 = first_query(layer, kb)
                for j in range(J):
                    mm = nc.tensor.matmul(ps_o[OROW * j:OROW * j + OROW, q0:T], vaug[:, g, kb, j, :],
                                          probs[:, kb % 2, j, q0:T], start=kb == 0, stop=kb == TT - 1)
                mm.then_inc(pv_done, 1)

            def body(turn):
                for u in range(QUADS):
                    g, kb = divmod(u, TT)
                    quad = QUADS * turn.job + u
                    group = turn.group_after(g, 2)
                    if kb == 0:
                        pe.wait_ge(shift_loaded, 16 * (G * turn.job + g + 1))
                    ahead = G * turn.job + g + 2
                    scores_t(turn.layer, g, kb, 0, J * quad)
                    scores_t(turn.layer, g, kb, 1, J * quad + 1)
                    if group:
                        scores(group[0], group[2], kb, 0, ahead, turn.job + (g >= 2))
                    step(turn, u, 0)
                    if group:
                        scores(group[0], group[2], kb, 1, ahead, turn.job + (g >= 2))
                    scores_t(turn.layer, g, kb, 2, J * quad + 2)
                    scores_t(turn.layer, g, kb, 3, J * quad + 3)
                    step(turn, u, 1)
                    if turn.job0 or u:
                        before = (u - 1) % QUADS
                        weigh_values(turn.layer if u else turn.tail_layer, before // TT, before % TT,
                                     quad - 1, G * turn.job + g - (kb == 0))

            pe.wait_ge(cast, 1)
            transpose_norm("A", 1, 0)
            pe.wait_ge(loaded["qkv_a"], 48)
            project_qk("A", 0, 1, even_bank)
            project_qk("A", 1, 1, odd_bank)
            project_v("A", 1)
            transpose_norm("A", 2, 1, norm_1_bank)
            project_qk("A", 0, 5, even_bank)
            project_qk("A", 1, 5, odd_bank)
            project_v("A", 5)
            for g in range(2):
                for qt in range(TT):
                    for pair in range(2):
                        scores(LA, g, qt, pair, g, 0)
                    if g == 1 and qt == 0:
                        transpose_max(0, PROLOGUE.index("shift_first"))
            pe.wait_ge(cast, CASTS)
            pe.wait_ge(loaded["rest"], 16 * REST_DMAS)
            turns(pe, body)
            weigh_values(LB, G - 1, TT - 1, QUADS * JOBS - 1, G * JOBS - 1)
            for u in range(QUADS, QUADS + 3):
                step(last_turn(), u, 0)
            last = LastTail()
            for name in TAIL_ORDER:
                number = last.number(name)
                if name == "out_proj":
                    out_proj(last, number)
                elif name == "norm_mid":
                    transpose_norm("mid", JOBS, number)
                elif name == "down":
                    down_proj(number)
                elif name.startswith("gate"):
                    project_hidden(wg, int(name[-1]), last.number("gate0"), gate_banks[int(name[-1])])
                else:
                    project_hidden(wu, int(name[-1]), last.number("gate0"), up_banks[int(name[-1])])

        @block.scalar
        def _(act):
            def copy_norm(kind, number, bank=ps_step[:, :]):
                act.wait_ge(step_written, number + 1)
                nc.scalar.copy(normed_t[kind][:, :], bank).then_inc(step_read, 1)

            def high_part_a(e, b, number, bank=ps_step[:, :]):
                act.wait_ge(step_written, number + 1)
                if not_met(16 * PARTS_DMAS * b):
                    act.wait_ge(parts_stored[LA], 16 * PARTS_DMAS * b)
                nc.scalar.activation(qk_parts["A"][:, 0, e, :], bank, ACT.Identity,
                                     bias=bqk[:, e:e + 1]).then_inc(high_done["A"], 1)

            def mid_part(kind, b, odd=None):
                if kind == "A":
                    act.wait_ge(step_read, odd + 1)
                else:
                    act.wait_ge(rest_done, b + 1)
                nc.scalar.copy(qk_parts[kind][:, 1, :, :], qk_rest[kind][:, :, :]).then_inc(mid_done[kind], 1)

            def raw_b(e, b, number):
                act.wait_ge(step_written, number + 1)
                act.wait_ge(rope_mul, 2 * b)
                nc.scalar.copy(qk_raw[:, e, :], ps_step[:, :]).then_inc(step_read, 1)

            def high_part_b(b):
                act.wait_ge(rope_done, 2 * (b + 1))
                act.wait_ge(parts_stored[LB], 16 * PARTS_DMAS * b)
                nc.scalar.copy(qk_parts["B"][:, 0, :, :], qk_rot[:, :, :]).then_inc(high_done["B"], 1)

            def copy_shift(number_of_group, number):
                act.wait_ge(step_written, number + 1)
                act.wait_ge(shift_loaded, 16 * number_of_group)
                nc.scalar.copy(shift_rows[:, :], ps_step_b[0:PARTS * J * TT, 0:128]).then_inc(step_read, 1)

            def tanh(job, hb, number, bank=ps_step[:, :]):
                act.wait_ge(step_written, number + 1)
                nc.scalar.activation(tanh_g[:, :], bank, ACT.Tanh, scale=0.5).then_inc(tanh_done, 1)

            def copy_o(g, job):
                act.wait_ge(pv_done, TT * (G * job + g + 1))
                if not_met(16 * O_DMAS * (2 * job + g // 2)):
                    act.wait_ge(o_moved[g % 2], 16 * O_DMAS * (2 * job + g // 2))
                if not_met(16 * (2 * job + g // 2)):
                    act.wait_ge(sums_moved[g % 2], 16 * (2 * job + g // 2))
                nc.scalar.copy(o_raw[:, g % 2, :], ps_o[:, :]).then_inc(o_copied, 1)

            def exp(layer, kb, j, quad):
                unit = J * quad + j
                q0 = first_query(layer, kb)
                act.wait_ge(st_ready, unit + 1)
                if j == 0:
                    if not_met(quad - 1):
                        act.wait_ge(pv_done, quad - 1)
                nc.scalar.activation(probs[:, kb % 2, j, q0:T], ps_t[j % 2][:, q0:T], ACT.Exp,
                                     scale=1.0 if layer == LA else float(DH) ** -0.5).then_inc(exp_done, 1)

            def step(turn, u, half):
                name = turn.steps.get((u, half))
                if name is not None:
                    number = turn.number(name)
                    if name == "norm_A":
                        copy_norm("A", number)
                    elif name == "norm_B":
                        copy_norm("B", number)
                    elif name == "norm_mid":
                        copy_norm("mid", number)
                    elif name == "qk_even_A":
                        high_part_a(0, turn.b_a, number)
                    elif name == "qk_odd_A":
                        high_part_a(1, turn.b_a, number)
                    elif name == "qk_even_B":
                        raw_b(0, turn.b_b, number)
                    elif name == "qk_odd_B":
                        raw_b(1, turn.b_b, number)
                    elif name.startswith("gate"):
                        tanh(turn.job - 1, int(name[-1]), number)
                    elif name.startswith("shift"):
                        copy_shift(G * turn.job + int(name[-1]) + 1, number)

            def body(turn):
                for u in range(QUADS):
                    g, kb = divmod(u, TT)
                    quad = QUADS * turn.job + u
                    exp(turn.layer, kb, 0, quad)
                    exp(turn.layer, kb, 1, quad)
                    if kb == 1 and (turn.job0 or g):
                        copy_o((g - 1) % G, turn.job - (g == 0))
                    step(turn, u, 0)
                    exp(turn.layer, kb, 2, quad)
                    exp(turn.layer, kb, 3, quad)
                    if u == 4 and turn.front_a:
                        mid_part("A", turn.b_a, turn.number("qk_odd_A"))
                    if u == HIGH_B_QUAD and turn.front_b:
                        high_part_b(turn.b_b)
                    if u == HIGH_B_QUAD + 2 and turn.front_b:
                        mid_part("B", turn.b_b)
                    step(turn, u, 1)

            act.wait_ge(half_filled, 1)
            nc.scalar.activation(exp_of_half[:, :], minus_half[:, :], ACT.Exp)
            act.wait_ge(loaded["qkv_a"], 48)
            copy_norm("A", 0)
            high_part_a(0, 0, 1, even_bank)
            high_part_a(1, 0, 2, odd_bank)
            mid_part("A", 0, 2)
            copy_norm("A", 4, norm_1_bank)
            high_part_a(0, 1, 5, even_bank)
            high_part_a(1, 1, 6, odd_bank)
            mid_part("A", 1, 6)
            copy_shift(0, PROLOGUE.index("shift_first"))
            turns(act, body)
            copy_o(G - 1, JOBS - 1)
            step(last_turn(), QUADS, 0)
            last = LastTail()
            copy_norm("mid", last.number("norm_mid"))
            for hb in range(HB):
                if hb:
                    act.wait_ge(step_read, last.number(f"gate{hb - 1}") + 1)
                tanh(JOBS - 1, hb, last.number(f"gate{hb}"), gate_banks[hb])

        @block.vector
        def _(dve):
            def norm_stats(kind, b, count):
                norm_stats_1(kind, b)
                norm_stats_2(kind, count)

            def norm_stats_1(kind, b):
                for i in range(TT):
                    op = nc.vector.bn_stats(stats[kind][:, i, :], x_all[:, b, i, :])
                op.then_inc(ln_stats[kind], 1)

            def norm_stats_2(kind, count):
                dve.wait_ge(ln_stats[kind], count)
                nc.vector.memset(wait_here[:, 0:1], 0.0)
                for i in range(TT):
                    op = nc.vector.bn_aggr(meanvar[kind][:, i, :], stats[kind][:, i, :])
                op.then_inc(ln_aggr[kind], 1)
                dve.wait_ge(ln_aggr[kind], count)
                nc.vector.tensor_scalar_add(var_eps[kind][:, :], meanvar[kind][:, :, 1], EPS).then_inc(ln_eps[kind], 1)

            def finish_norm(kind, b, rstd_count):
                dve.wait_ge(ln_rstd[kind], rstd_count)
                for i in range(TT):
                    op = nc.vector.tensor_scalar(normed[kind][:, i, :], x_all[:, b, i, :],
                                                 meanvar[kind][:, i, 0:1], rstd[kind][:, i, :],
                                                 op0=ALU.subtract, op1=ALU.mult)
                op.then_inc(ln_done[kind], 1)

            def rest_part_a(e, b, bank=ps_step[:, :]):
                dve.wait_ge(high_done["A"], 2 * b + e + 1)
                if not_met(b):
                    dve.wait_ge(low_done["A"], b)
                nc.vector.scalar_tensor_tensor(out=qk_rest["A"][:, e, :], in0=bank, scalar=bqk[:, e:e + 1],
                                               in1=qk_parts["A"][:, 0, e, :], op0=ALU.add,
                                               op1=ALU.subtract).then_inc(step_read, 1)

            def copy_v(layer, b, number):
                dve.wait_ge(step_written, number + 1)
                dst = v_all[:, b, :, :]
                src = ps_step[:, :].rearrange("p (i d) -> p i d", i=TT)
                if layer == LA:
                    op = nc.vector.tensor_tensor(dst, src, bv[:, :].unsqueeze(1).broadcast_to([128, TT, D]), ALU.add)
                else:
                    dve.wait_ge(vaug_copied, G * (b + 1))
                    op = nc.vector.tensor_copy(dst, src)
                op.then_inc(step_read, 1)

            def split_maxima(number_of_group):
                before = 4 * number_of_group
                high, mid, low = (negmax_parts[:, n, :, :] for n in range(PARTS))
                dve.wait_ge(max_done, 2 * TT * (number_of_group + 1))
                nc.vector.tensor_copy(high, negmax[:, :, :]).then_inc(shift_split, 1)
                dve.wait_ge(shift_split, before + 1)
                nc.vector.tensor_tensor(negmax_rest[:, :, :], negmax[:, :, :], high, ALU.subtract).then_inc(shift_split, 1)
                dve.wait_ge(shift_split, before + 2)
                nc.vector.tensor_copy(mid, negmax_rest[:, :, :]).then_inc(shift_split, 1)
                dve.wait_ge(shift_split, before + 3)
                nc.vector.tensor_tensor(low, negmax_rest[:, :, :], mid, ALU.subtract).then_inc(shift_split, 1)

            def residual(b, number):
                dve.wait_ge(step_written, number + 1)
                nc.vector.tensor_tensor(x_all[:, b, :, :], ps_step[:, :].rearrange("p (i d) -> p i d", i=TT),
                                        x_all[:, b, :, :], ALU.add).then_inc(step_read, 1)
                dve.wait_ge(x_first, 16)
                dve.wait_ge(step_read, number + 1)

            def gate(job, hb, bank=ps_step[:, :]):
                count = HB * job + hb + 1
                dve.wait_ge(tanh_done, count)
                nc.vector.scalar_tensor_tensor(out=gate_act[:, :], in0=tanh_g[:, :], scalar=1.0, in1=bank,
                                               op0=ALU.add, op1=ALU.mult).then_inc(step_read, 1)

            def up(hb, number, bank=ps_step[:, :]):
                dve.wait_ge(step_written, number + 1)
                nc.vector.tensor_tensor(hidden[:, hb, :], bank, gate_act[:, :], ALU.mult).then_inc(step_read, 1)

            def reciprocals(job):
                for half in range(2):
                    dve.wait_ge(sums_moved[half], 16 * (G // 2) * (job + 1))
                nc.vector.reciprocal(recips[:, :], sums[:, :]).then_inc(recip_done, 1)

            def maxima(layer, g, i, pair, number):
                qt = query_tile(layer, i)
                keys = last_key(layer, qt)
                dve.wait_ge(s_ready, number + 1)
                nc.vector.tensor_reduce(negmax[:, 2 * pair:2 * pair + 2, qt], ps_s[pair][:, :, 0:keys],
                                        AX.X, ALU.max, negate=True).then_inc(max_done, 1)

            def step(turn, u, half):
                name = turn.steps.get((u, half))
                if name is not None:
                    number = turn.number(name)
                    if name == "qk_even_A":
                        rest_part_a(0, turn.b_a)
                    elif name == "qk_odd_A":
                        rest_part_a(1, turn.b_a)
                    elif name == "v_A":
                        copy_v(LA, turn.b_a, number)
                    elif name == "v_B":
                        copy_v(LB, turn.b_b, number)
                    elif name == "out_proj":
                        residual(turn.tail_b, number)
                        norm_stats_1("mid", turn.tail_b)
                    elif name == "down":
                        residual(turn.tail_b, number)
                    elif name.startswith("gate"):
                        gate(turn.job - 1, int(name[-1]))
                    elif name.startswith("up"):
                        up(int(name[-1]), number)

            def body(turn):
                for u in range(QUADS):
                    g, kb = divmod(u, TT)
                    group = turn.group_after(g, 2)
                    pairs = 2 * (QUADS * turn.job + u + 2 * TT)
                    if u == 0 and turn.front_a:
                        norm_stats_1("A", turn.b_a)
                    if group:
                        maxima(group[0], group[2], kb, 0, pairs)
                    if turn.tail and turn.layer == LA and u == 6:
                        norm_stats_2("mid", turn.job)
                    step(turn, u, 0)
                    if u == 0 and turn.front_a:
                        norm_stats_2("A", turn.b_a + 1)
                    if turn.front_b and u == 2:
                        norm_stats_1("B", turn.b_b)
                    elif turn.front_b and u == 3:
                        norm_stats_2("B", turn.b_b + 1)
                    if u == RECIP_QUAD[turn.layer] and turn.tail:
                        reciprocals(turn.job - 1)
                    if group:
                        maxima(group[0], group[2], kb, 1, pairs + 1)
                        if kb == TT - 1:
                            split_maxima(G * turn.job + g + 2)
                    if turn.tail and turn.layer == LB and u == 6:
                        norm_stats_2("mid", turn.job)
                    step(turn, u, 1)

            dve.wait_ge(x_first, 16)
            norm_stats("A", 0, 1)
            finish_norm("A", 0, 1)
            nc.vector.memset(negmax_cols[:, :].bitcast(F32), 0.0)
            dve.wait_ge(loaded["ident"], 16)
            nc.vector.tensor_copy(identb[:, :], identf[:, :]).then_inc(cast, 1)
            nc.vector.memset(qr[:, :, :, :].rearrange("p g j t -> p (g j t)").bitcast(F32), 0.0).then_inc(q_zeroed, 1)
            dve.wait_ge(loaded["qkv_a"], 48)
            rest_part_a(0, 0, even_bank)
            rest_part_a(1, 0, odd_bank)
            dve.wait_ge(x_second, 16)
            norm_stats_1("A", 1)
            dve.wait_ge(mid_done["A"], 1)
            nc.vector.tensor_tensor(qk_parts["A"][:, 2, :, :], qk_rest["A"][:, :, :], qk_parts["A"][:, 1, :, :],
                                    ALU.subtract).then_inc(low_done["A"], 1)
            copy_v(LA, 0, 3)
            norm_stats_2("A", 2)
            dve.wait_ge(loaded["rest"], 16 * REST_DMAS)
            for dst, src, scale in ((wg, w_int[0], WSCALE), (wu, w_int[1], WSCALE), (wd, w_int[2], 0.5 * WSCALE)):
                nc.vector.tensor_scalar(dst[:, :], src[:, :], scale, None, ALU.mult).then_inc(cast, 1)
            nc.vector.tensor_copy(masks_b[:, :, :], masks_f[:, :, :]).then_inc(cast, 1)
            rest_part_a(0, 1, even_bank)
            rest_part_a(1, 1, odd_bank)
            copy_v(LA, 1, 7)
            for g in range(2):
                for qt in range(TT):
                    for pair in range(2):
                        maxima(LA, g, qt, pair, 2 * TT * g + 2 * qt + pair)
                split_maxima(g)
            dve.wait_ge(x_others, 16)
            turns(dve, body)
            step(last_turn(), QUADS, 0)
            reciprocals(JOBS - 1)
            step(last_turn(), QUADS + 1, 0)
            step(last_turn(), QUADS + 2, 0)
            for half in range(2):
                dve.wait_ge(o_moved[half], 16 * O_DMAS * (G // 2) * JOBS)
            dve.wait_ge(recip_loaded, 16 * JOBS)
            nc.vector.tensor_tensor(attn_t[:, :], o_cols[:, :], recip_cols[:, :], ALU.mult).then_inc(attn_scaled, 1)
            last = LastTail()
            residual(NB - 1, last.number("out_proj"))
            norm_stats("mid", NB - 1, JOBS)
            finish_norm("mid", NB - 1, 2 * (JOBS - 1) + 1)
            for hb in range(HB):
                if hb:
                    dve.wait_ge(step_read, last.number(f"up{hb - 1}") + 1)
                gate(JOBS - 1, hb, gate_banks[hb])
                dve.wait_ge(step_read, last.number(f"gate{hb}") + 1)
                up(hb, last.number(f"up{hb}"), up_banks[hb])
            residual(NB - 1, last.number("down"))

        @block.gpsimd
        def _(pool):
            def inverse_deviation(kind, count):
                pool.wait_ge(ln_eps[kind], count)
                nc.gpsimd.tensor_tensor(rstd[kind][:, :, 0], var_eps[kind][:, :], minus_half[:, :],
                                        ALU.pow).then_inc(ln_rstd[kind], 1)

            def norm_1(kind, b, count):
                inverse_deviation(kind, count)
                mean = meanvar[kind][:, :, 0:1].broadcast_to([128, TT, D])
                nc.gpsimd.tensor_tensor(centred[kind][:, :, :], x_all[:, b, :, :], mean,
                                        ALU.subtract).then_inc(ln_rstd[kind], 1)

            def norm_2(kind, count):
                pool.wait_ge(ln_rstd[kind], 2 * count - (kind == "A"))
                nc.gpsimd.tensor_tensor(normed[kind][:, :, :], centred[kind][:, :, :],
                                        rstd[kind][:, :, :].broadcast_to([128, TT, D]),
                                        ALU.mult).then_inc(ln_done[kind], 1)

            def add_bias(b):
                nc.gpsimd.tensor_tensor(x_all[:, b, :, :], x_all[:, b, :, :],
                                        bout[:, :].unsqueeze(1).broadcast_to([128, TT, D]),
                                        ALU.add).then_inc(bias_added, 1)

            def copy_values(group, number):
                layer, b, g = group
                if not_met(TT * (number - G + 1)):
                    pool.wait_ge(pv_done, TT * (number - G + 1))
                src = v_all[:, b, :, J * DH * g:J * DH * (g + 1)].rearrange("p i (j d) -> p i j d", j=J)
                nc.gpsimd.tensor_copy(vaug[:, g, :, :, 0:DH], src).then_inc(vaug_copied, 1)

            def low_part(kind, b):
                pool.wait_ge(mid_done[kind], b + 1)
                nc.gpsimd.tensor_tensor(qk_parts[kind][:, 2, :, :], qk_rest[kind][:, :, :], qk_parts[kind][:, 1, :, :],
                                        ALU.subtract).then_inc(low_done[kind], 1)

            def rope_1(b, odd):
                pool.wait_ge(step_read, odd + 1)
                both = [128, 2, T]
                nc.gpsimd.tensor_tensor(by_cos[:, :, :], qk_raw[:, :, :], cosines[:, :].unsqueeze(1).broadcast_to(both),
                                        ALU.mult).then_inc(rope_mul, 1)
                nc.gpsimd.tensor_tensor(by_sin[:, :, :], qk_raw[:, :, :], sines[:, :].unsqueeze(1).broadcast_to(both),
                                        ALU.mult).then_inc(rope_mul, 1)

            def rope_2(b):
                pool.wait_ge(rope_mul, 2 * (b + 1))
                nc.gpsimd.tensor_tensor(qk_rot[:, 0, :], by_cos[:, 0, :], by_sin[:, 1, :],
                                        ALU.subtract).then_inc(rope_done, 1)
                nc.gpsimd.tensor_tensor(qk_rot[:, 1, :], by_sin[:, 0, :], by_cos[:, 1, :],
                                        ALU.add).then_inc(rope_done, 1)

            def rest_part_b(b):
                pool.wait_ge(high_done["B"], b + 1)
                nc.gpsimd.tensor_tensor(qk_rest["B"][:, :, :], qk_rot[:, :, :], qk_parts["B"][:, 0, :, :],
                                        ALU.subtract).then_inc(rest_done, 1)

            def scale_attn(job):
                for half in range(2):
                    pool.wait_ge(o_moved[half], 16 * O_DMAS * (G // 2) * (job + 1))
                pool.wait_ge(recip_loaded, 16 * (job + 1))
                nc.gpsimd.tensor_tensor(attn_t[:, :], o_cols[:, :], recip_cols[:, :], ALU.mult).then_inc(attn_scaled, 1)

            def body(turn):
                first = G * turn.job
                late = turn.layer == LB
                if turn.front_a:
                    norm_1("A", turn.b_a, turn.b_a + 1)
                    norm_2("A", turn.b_a + 1)
                    add_bias(turn.b_a)
                for u in range(QUADS):
                    g, kb = divmod(u, TT)
                    group = turn.group_after(g, 3)
                    if kb == 1 and group:
                        copy_values(group, first + g + 3)
                    if turn.front_b:
                        if u == 3:
                            norm_1("B", turn.b_b, turn.b_b + 1)
                        elif u == 4:
                            norm_2("B", turn.b_b + 1)
                        elif u == 11:
                            rest_part_b(turn.b_b)
                        elif u == 14:
                            low_part("B", turn.b_b)
                            pool.wait_ge(step_read, turn.number("v_B") + 1)
                    if turn.tail:
                        if u == (5 if late else 3):
                            scale_attn(turn.job - 1)
                        elif u == 6:
                            norm_1("mid", turn.tail_b, turn.job)
                        elif u == 7:
                            norm_2("mid", turn.job)
                    if turn.front_b:
                        if u == (9 if late else 8):
                            rope_1(turn.b_b, turn.number("qk_odd_B"))
                        elif u == (10 if late else 9):
                            rope_2(turn.b_b)
                    if u == 5 and turn.front_a:
                        low_part("A", turn.b_a)
                        pool.wait_ge(step_read, turn.number("v_A") + 1)

            nc.gpsimd.memset(minus_half[:, :], -0.5).then_inc(half_filled, 1)
            pool.wait_ge(half_filled, 1)
            inverse_deviation("A", 1)
            kr_words = kr[:, :, :, :].rearrange("p g j t -> p (g j t)").bitcast(F32)
            nc.gpsimd.memset(kr_words, 0.0).then_inc(k_filled, 1)
            pool.wait_ge(k_filled, 1)
            nc.gpsimd.memset(kr_words[SH:128, :], TWO_ONES).then_inc(k_filled, 1)
            pool.wait_ge(k_filled, 2)
            norm_1("A", 1, 2)
            norm_2("A", 2)
            nc.gpsimd.memset(vaug[:, :, :, :, :], 0.0).then_inc(vaug_filled, 1)
            pool.wait_ge(vaug_filled, 1)
            nc.gpsimd.memset(vaug[:, :, :, :, SUMROW:SUMROW + 1], 1.0).then_inc(vaug_filled, 1)
            pool.wait_ge(vaug_filled, 2)
            pool.wait_ge(step_read, 4)
            for g in range(3):
                copy_values((LA, 0, g), g)
            low_part("A", 1)
            pool.wait_ge(step_read, 8)
            pool.wait_ge(loaded["rest"], 16 * REST_DMAS)
            add_bias(0)
            add_bias(1)
            turns(pool, body)
            inverse_deviation("mid", JOBS)


_NAMES = ["x", "w_qkv_a", "b_qk_a", "b_v_a", "w_out_a", "b_out_a", "w_qkv_b", "w_out_b",
          "w_gate", "w_up", "w_down", "ident", "mask_s", "mask_t", "rope_cos", "rope_sin"]


def _by_pairs(w):
    return w.reshape(w.shape[0], H, HALF, 2).transpose(0, 3, 2, 1).reshape(w.shape[0], 2, HALF * H)


def _qkv(wq, wk, wv):
    q, k = _by_pairs(wq), _by_pairs(wk)
    return np.ascontiguousarray(np.stack([np.concatenate([q[:, 0], k[:, 0]], 1),
                                          np.concatenate([q[:, 1], k[:, 1]], 1), wv], 1))


def _rope_tables():
    powers = np.arange(0, DH, 2, dtype=np.float32) / np.float32(DH)
    freqs = (np.float32(1.0) / np.float32(10000.0) ** powers).astype(np.float32)
    angles = np.outer(np.arange(T, dtype=np.float32), freqs).T[None, :, None, :]
    rows = np.broadcast_to(angles, (2, HALF, H, T)).reshape(128, T)
    return np.cos(rows).astype(np.float32), np.sin(rows).astype(np.float32)


def kernel(L0_attn_a_x, L0_attn_a_w1, L0_attn_a_b1, L0_attn_a_w2, L0_attn_a_b2, L0_attn_b_wq, L0_attn_b_wk,
           L0_attn_b_wv, L0_attn_b_wo, L0_ffn_w_gate, L0_ffn_w_up, L0_ffn_w_down):
    import concourse.bacc as _bacc
    from concourse.bass_utils import run_bass_kernel_spmd as _run

    w1, b1 = np.asarray(L0_attn_a_w1), np.asarray(L0_attn_a_b1)
    bq, bk = _by_pairs(b1[None, 0:D])[0], _by_pairs(b1[None, D:2 * D])[0]
    wd = np.asarray(L0_ffn_w_down)
    cos, sin = _rope_tables()
    later = np.arange(128)[None, :] > np.arange(128)[:, None]
    mask_s = np.where(later, np.float32(BIG), np.float32(0.0))
    arrays = dict(
        x=np.asarray(L0_attn_a_x),
        w_qkv_a=_qkv(w1[:, 0:D], w1[:, D:2 * D], w1[:, 2 * D:3 * D]),
        b_qk_a=np.concatenate([bq, bk], 1).T,
        b_v_a=b1[2 * D:3 * D],
        w_out_a=np.asarray(L0_attn_a_w2),
        b_out_a=np.asarray(L0_attn_a_b2),
        w_qkv_b=_qkv(np.asarray(L0_attn_b_wq).T, np.asarray(L0_attn_b_wk).T, np.asarray(L0_attn_b_wv).T),
        w_out_b=np.asarray(L0_attn_b_wo).T,
        w_gate=np.asarray(L0_ffn_w_gate).T,
        w_up=np.asarray(L0_ffn_w_up).T,
        w_down=wd.T.reshape(HB, 128, D).transpose(1, 0, 2).reshape(128, HB * D),
        ident=np.eye(128, dtype=np.float32),
        mask_s=mask_s, mask_t=mask_s.T, rope_cos=cos, rope_sin=sin)
    nc = _bacc.Bacc("TRN2", target_bir_lowering=False, num_devices=1)
    ins, args = {}, []
    for name in _NAMES:
        a = np.ascontiguousarray(arrays[name])
        ins[f"in_{name}"] = a
        args.append(nc.dram_tensor(f"in_{name}", a.shape, mybir.dt.from_np(a.dtype), kind="ExternalInput").ap())
    out = nc.dram_tensor("out_x", (NB, T, D), F32, kind="ExternalOutput").ap()
    hybrid_block_kernel(nc, *args, out)
    r = _run(nc, [ins], core_ids=[0])
    return r.results[0]["out_x"]
```
